# Optimizing a Trainium2 kernel written in Bass

```python
import numpy as np
import jax
import jax.numpy as jnp

def _softmax(x, axis=-1):
    return jax.nn.softmax(x, axis=axis)
def _gelu(x):
    return jax.nn.gelu(x, approximate=True)
def _silu(x):
    return jax.nn.silu(x)
def _sigmoid(x):
    return jax.nn.sigmoid(x)
def _layernorm(x, axis=-1, eps=1e-5):
    m = jnp.mean(x, axis=axis, keepdims=True)
    v = jnp.var(x, axis=axis, keepdims=True)
    return (x - m) / jnp.sqrt(v + eps)
def _scatter_add(tgt, idx, src, axis=0):
    return tgt.at[idx].add(src)
def _segment_sum(src, seg, n):
    return jax.ops.segment_sum(src, seg, n)

kernel_name = 'mk_adj_preln_d2_adj_256_c91f43'

def setup_inputs(seed: int = 0):
    np.random.seed(seed)
    _w = jnp.asarray
    def _rec_inputs():
        import jax
        import jax.numpy as jnp
        _gk = jax.random.key(seed)
        x = -0.0002928 + 1 * jax.random.normal(jax.random.fold_in(_gk, 1), (16, 1024, 256), jnp.float32)
        _w = (1.0 + jnp.arange(1024, dtype=jnp.float32)) ** -0.5
        _w = _w / _w.mean()
        _pij = jnp.clip(0.03125 * _w[:, None] * _w[None, :], 0.0, 1.0)
        _a = jax.random.uniform(jax.random.fold_in(_gk, 2), (16, 1024, 1024)) < _pij
        adj = _a.astype(jnp.int32)
        return x, adj
    x, adj = _rec_inputs()
    def _L0_gnn_setup():
        import jax, jax.numpy as jnp
        import numpy as np
        LEAKY_SLOPE = 0.2
        NEG_INF = -9000000000000000.0

        def _edge_scores(h, a_k):
            e = jnp.einsum('bid,bjd->bij', h * a_k[:, 0], h)
            return jax.nn.leaky_relu(e, negative_slope=LEAKY_SLOPE)
        key = jax.random.key(seed)
        k1, k2, k3, k4, k5, k6 = jax.random.split(key, 6)
        B, N, D = (32, 512, 256)
        hidden = jax.random.normal(k1, (B, N, D), dtype=jnp.float32)
        adj = jax.random.randint(k2, (B, N, N), 0, 5, dtype=jnp.int32)
        a_0 = jax.random.normal(k3, (D, 1), dtype=jnp.float32)
        a_1 = jax.random.normal(k4, (D, 1), dtype=jnp.float32)
        a_2 = jax.random.normal(k5, (D, 1), dtype=jnp.float32)
        a_3 = jax.random.normal(k6, (D, 1), dtype=jnp.float32)
        return {'hidden': hidden, 'adj': adj, 'a_0': a_0, 'a_1': a_1, 'a_2': a_2, 'a_3': a_3}
    _L0_gnn_all = _L0_gnn_setup()
    _L0_gnn_in = {k: v for k, v in _L0_gnn_all.items() if k in ('a_0', 'a_1', 'a_2', 'a_3', )}
    del _L0_gnn_all

    def _L1_gnn_setup():
        import jax, jax.numpy as jnp
        import numpy as np
        B, N, D = (8, 1024, 256)
        H, HO = (4, 64)
        T = 5
        NEG = -1000000000.0
        EPS = 1e-06
        key = jax.random.key(seed)
        ks = jax.random.split(key, 6)
        nodes_embed = jax.random.normal(ks[0], (B, N, D), dtype=jnp.float32)
        node_adj = jax.random.randint(ks[1], (B, N, N), 0, T + 1)
        W = jax.random.normal(ks[2], (H, D, HO), dtype=jnp.float32) * (1.0 / np.sqrt(D))
        a_src = jax.random.normal(ks[3], (H, T, HO), dtype=jnp.float32) * 0.1
        a_dst = jax.random.normal(ks[4], (H, T, HO), dtype=jnp.float32) * 0.1
        bias = jnp.zeros((H, HO), dtype=jnp.float32)
        ln_gamma = jnp.ones((H, HO), dtype=jnp.float32)
        ln_beta = jnp.zeros((H, HO), dtype=jnp.float32)
        return {'nodes_embed': nodes_embed, 'node_adj': node_adj, 'W': W, 'a_src': a_src, 'a_dst': a_dst, 'bias': bias, 'ln_gamma': ln_gamma, 'ln_beta': ln_beta}
    _L1_gnn_all = _L1_gnn_setup()
    _L1_gnn_in = {k: v for k, v in _L1_gnn_all.items() if k in ('W', 'a_src', 'a_dst', 'bias', 'ln_gamma', 'ln_beta', )}
    del _L1_gnn_all

    return {
        "x": x,
        "adj": adj,
        "L0_gnn_a_0": _L0_gnn_in["a_0"],
        "L0_gnn_a_1": _L0_gnn_in["a_1"],
        "L0_gnn_a_2": _L0_gnn_in["a_2"],
        "L0_gnn_a_3": _L0_gnn_in["a_3"],
        "L1_gnn_W": _L1_gnn_in["W"],
        "L1_gnn_a_src": _L1_gnn_in["a_src"],
        "L1_gnn_a_dst": _L1_gnn_in["a_dst"],
        "L1_gnn_bias": _L1_gnn_in["bias"],
        "L1_gnn_ln_gamma": _L1_gnn_in["ln_gamma"],
        "L1_gnn_ln_beta": _L1_gnn_in["ln_beta"],
    }

def reference(x, adj, L0_gnn_a_0, L0_gnn_a_1, L0_gnn_a_2, L0_gnn_a_3, L1_gnn_W, L1_gnn_a_src, L1_gnn_a_dst, L1_gnn_bias, L1_gnn_ln_gamma, L1_gnn_ln_beta):
    import jax
    import jax.numpy as jnp
    def _L0_gnn_ref(hidden, adj, a_0, a_1, a_2, a_3):
        import jax, jax.numpy as jnp
        import numpy as np
        LEAKY_SLOPE = 0.2
        NEG_INF = -9000000000000000.0

        def _edge_scores(h, a_k):
            e = jnp.einsum('bid,bjd->bij', h * a_k[:, 0], h)
            return jax.nn.leaky_relu(e, negative_slope=LEAKY_SLOPE)
        h = hidden
        e_0 = _edge_scores(h, a_0)
        e_1 = _edge_scores(h, a_1)
        e_2 = _edge_scores(h, a_2)
        e_3 = _edge_scores(h, a_3)
        scores = jnp.where(adj == 1, e_0, NEG_INF)
        scores = jnp.where(adj == 2, e_1, scores)
        scores = jnp.where(adj == 3, e_2, scores)
        scores = jnp.where(adj == 4, e_3, scores)
        alpha = jax.nn.softmax(scores, axis=-1)
        return jnp.einsum('bij,bjd->bid', alpha, h)

    def _L1_gnn_ref(nodes_embed, node_adj, W, a_src, a_dst, bias, ln_gamma, ln_beta):
        import jax, jax.numpy as jnp
        import numpy as np
        B, N, D = (8, 1024, 256)
        H, HO = (4, 64)
        T = 5
        NEG = -1000000000.0
        EPS = 1e-06
        h = jnp.einsum('bnd,hde->bhne', nodes_embed, W)
        e_src = jnp.einsum('bhne,hte->bhtn', h, a_src)
        e_dst = jnp.einsum('bhne,hte->bhtn', h, a_dst)
        n_types = a_src.shape[1]
        weight = jnp.zeros(h.shape[:2] + (h.shape[2], h.shape[2]), dtype=h.dtype)
        for t in range(n_types):
            mask = (node_adj == t + 1).astype(h.dtype)[:, None]
            weight = weight + mask * (e_src[:, :, t, :, None] + e_dst[:, :, t, None, :])
        weight = jax.nn.leaky_relu(weight, negative_slope=0.01)
        weight = jnp.where(node_adj[:, None] == 0, NEG, weight)
        attention = jax.nn.softmax(weight, axis=-1)
        dst = jnp.einsum('bhij,bhje->bhie', attention, h) + bias[None, :, None, :]
        out = jax.nn.relu(dst) + h
        mu = out.mean(axis=-1, keepdims=True)
        var = out.var(axis=-1, keepdims=True)
        out = (out - mu) / jnp.sqrt(var + EPS) * ln_gamma[None, :, None, :] + ln_beta[None, :, None, :]
        b, hh, n, e = out.shape
        return out.transpose(0, 2, 1, 3).reshape(b, n, hh * e)

    h = jnp.maximum(_layernorm(x, axis=-1), 0.0)
    x = x + _L0_gnn_ref(h, adj, L0_gnn_a_0, L0_gnn_a_1, L0_gnn_a_2, L0_gnn_a_3)
    h = jnp.maximum(_layernorm(x, axis=-1), 0.0)
    x = x + _L1_gnn_ref(h, adj, L1_gnn_W, L1_gnn_a_src, L1_gnn_a_dst, L1_gnn_bias, L1_gnn_ln_gamma, L1_gnn_ln_beta)
    return x


_drawn_inputs = setup_inputs


def setup_inputs(seed=0):
    import zlib

    import numpy as np

    out = dict(_drawn_inputs(seed))
    spreads = {'L1_gnn_bias': (0.0, 0.1), 'L1_gnn_ln_gamma': (1.0, 0.2), 'L1_gnn_ln_beta': (0.0, 0.1)}
    factors = {'L1_gnn_a_src': 11.089}
    for name, (base, spread) in spreads.items():
        noise = np.random.default_rng([zlib.crc32(name.encode()), seed]).standard_normal(out[name].shape)
        drawn = base * np.exp(spread * noise) if base else spread * noise
        out[name] = jnp.asarray(drawn.astype(out[name].dtype))
    for name, factor in factors.items():
        out[name] = (out[name] * factor).astype(out[name].dtype)
    return out
```

```python
from contextlib import ExitStack

import concourse.bass as bass
from concourse import mybir

ALU = mybir.AluOpType
ACT = mybir.ActivationFunctionType
F32 = mybir.dt.float32
BF16 = mybir.dt.bfloat16
I32 = mybir.dt.int32
U8 = mybir.dt.uint8
AX_X = mybir.AxisListType.X

P = 128
B, N, D = 16, 1024, 256
R = N // P
C = D // P
K0 = 4
H, E, T1 = 4, 64, 5
HT = H * T1
WN = D + 2 * HT
LN_EPS = 1e-5
HEAD_EPS = 1e-6
SLOPE0, SLOPE1 = 0.2, 0.01
NEG0, NEG1 = -9000000000000000.0, -1000000000.0


class Steps:

    def __init__(self, eng, sem, start=0):
        self.eng, self.sem, self.start, self.n = eng, sem, start, 0

    def did(self, ins):
        ins.then_inc(self.sem, 1)
        self.n += 1

    def settle(self):
        self.eng.wait_ge(self.sem, self.start + self.n)


def constants(nc, ctx, ins):
    sb = lambda name, shape, dt: ctx.enter_context(nc.sbuf_tensor(name, shape, dt))
    sem = lambda name: ctx.enter_context(nc.semaphore(name))
    k = {
        "ident": sb("ident", [P, P], F32),
        "aT": sb("aT", [P, C, K0], F32),
        "wa": sb("wa", [P, C, WN], F32),
        "sel": sb("sel", [2 * HT, HT, P], F32),
        "bgb": sb("bgb", [P, 3, D], F32),
        "eps": sb("eps", [P, 2], F32),
    }
    ident, aT, wa, sel, bgb, eps = (k[n] for n in ("ident", "aT", "wa", "sel", "bgb", "eps"))
    with ExitStack() as own:
        tb = lambda name, shape, dt: own.enter_context(nc.sbuf_tensor(name, shape, dt))
        pb = lambda name, shape: own.enter_context(nc.psum_tensor(name, shape, F32))
        sm = lambda name: own.enter_context(nc.semaphore(name))
        attn_rows = tb("attn_rows", [2 * HT, E], F32)
        attn_cols = tb("attn_cols", [E, 2 * HT], F32)
        wT = tb("wT", [E, H, D], F32)
        rows = tb("rows", [1, 3, D], F32)
        ones = tb("ones", [1, P], F32)
        ps_wT = pb("ps_wT", [P, 2, 512])
        ps_wa = pb("ps_wa", [P, C, 2 * HT])
        ps_rows = pb("ps_rows", [P, 2, 512])
        ps_at = pb("ps_at", [P, 512])
        w_in, rows_in, attn_in = sm("w_in"), sm("rows_in"), sm("attn_in")
        filled, ident_ready, turned, turned_out, folded, spread = (
            sm(n) for n in ("filled", "ident_ready", "turned", "turned_out", "folded", "spread"))
        block = own.enter_context(nc.Block())

        @block.sync
        def _(sp):
            for h in range(H):
                sp.dma_start(wa[:, :, h * E:(h + 1) * E],
                             ins["L1_gnn_W"][h].rearrange("(c p) e -> p c e", p=P)).then_inc(w_in, 16)
            for k_, name in enumerate(["L0_gnn_a_0", "L0_gnn_a_1", "L0_gnn_a_2", "L0_gnn_a_3"]):
                sp.dma_start(aT[:, :, k_:k_ + 1],
                             ins[name].rearrange("(c p) o -> p c o", p=P),
                             allow_slow_non_contiguous=True).then_inc(w_in, 16)
            sp.wait_ge(w_in, 16 * (H + K0))

        @block.scalar
        def _(act):
            for i, name in enumerate(["L1_gnn_a_src", "L1_gnn_a_dst"]):
                act.dma_start(attn_rows[i * HT:(i + 1) * HT, :],
                              ins[name].rearrange("h t e -> (h t) e")).then_inc(attn_in, 16)
            for i, name in enumerate(["L1_gnn_bias", "L1_gnn_ln_gamma", "L1_gnn_ln_beta"]):
                act.dma_start(rows[:, i, :], ins[name].rearrange("(o h) e -> o (h e)", o=1)).then_inc(rows_in, 16)
            act.wait_ge(rows_in, 48)

        @block.gpsimd
        def _(pool):
            pool.memset(ident[:], 0.0).then_inc(filled, 1)
            pool.memset(sel[:], 0.0).then_inc(filled, 1)
            pool.memset(ones[:], 1.0).then_inc(filled, 1)
            pool.memset(eps[:, 0:1], LN_EPS).then_inc(filled, 1)
            pool.memset(eps[:, 1:2], HEAD_EPS).then_inc(filled, 1)
            pool.wait_ge(filled, 5)
            pool.affine_select(out=ident[:], in_=ident[:], compare_op=ALU.not_equal, fill=1.0, base=0,
                               pattern=[[-1, P]], channel_multiplier=1).then_inc(ident_ready, 1)
            pool.affine_select(out=sel[:], in_=sel[:], compare_op=ALU.not_equal, fill=1.0, base=-HT,
                               pattern=[[-1, HT], [0, P]], channel_multiplier=1).then_inc(ident_ready, 1)
            pool.wait_ge(ident_ready, 2)

        @block.tensor
        def _(pe):
            pe.wait_ge(ident_ready, 2)
            pe.wait_ge(w_in, 16 * (H + K0))
            pe.wait_ge(attn_in, 32)
            for h in range(H):
                for c in range(C):
                    last = pe.transpose(ps_wT[0:E, h // 2, (h % 2) * D + c * P:(h % 2) * D + (c + 1) * P],
                                        wa[:, c, h * E:(h + 1) * E], ident[:])
            last = pe.transpose(ps_at[0:E, 0:2 * HT], attn_rows[:], ident[0:2 * HT, 0:2 * HT])
            last.then_inc(turned, 1)
            pe.wait_ge(rows_in, 48)
            pe.wait_ge(filled, 5)
            flat = rows[:, :, :].rearrange("p a d -> p (a d)")
            pe.matmul(ps_rows[:, 0, :], ones[:], flat[:, 0:512], start=True, stop=True)
            pe.matmul(ps_rows[:, 1, 0:D], ones[:], flat[:, 512:768], start=True, stop=True).then_inc(spread, 1)
            pe.wait_ge(turned_out, 2)
            for c in range(C):
                for h in range(H):
                    for s in range(2):
                        col = s * HT + h * T1
                        last = pe.matmul(ps_wa[:, c, col:col + T1], wT[:, h, c * P:(c + 1) * P],
                                         attn_cols[:, col:col + T1], start=True, stop=True)
            last.then_inc(folded, 1)

        @block.vector
        def _(dve):
            dve.wait_ge(turned, 1)
            dve.tensor_copy(wT[:].rearrange("p (a b) d -> p a (b d)", a=2), ps_wT[0:E, :, :]).then_inc(turned_out, 1)
            dve.tensor_copy(attn_cols[:], ps_at[0:E, 0:2 * HT]).then_inc(turned_out, 1)
            dve.wait_ge(spread, 1)
            flat = bgb[:].rearrange("p a d -> p (a d)")
            dve.tensor_copy(flat[:, 0:512], ps_rows[:, 0, :])
            dve.tensor_copy(flat[:, 512:768], ps_rows[:, 1, 0:D])
            dve.wait_ge(folded, 1)
            dve.tensor_copy(wa[:, :, D:WN], ps_wa[:])
    return k


def general_path(nc, k, ins, out, flag):
    x, adj = ins["x"], ins["adj"]
    ident, aT, wa, sel, bgb, eps = (k[n] for n in ("ident", "aT", "wa", "sel", "bgb", "eps"))
    with ExitStack() as ctx:
        sb = lambda name, shape, dt: ctx.enter_context(nc.sbuf_tensor("g_" + name, shape, dt))
        pb = lambda name, shape: ctx.enter_context(nc.psum_tensor("g_" + name, shape, F32))
        sem = lambda name: ctx.enter_context(nc.semaphore("g_" + name))
        xs = sb("xs", [P, R, D], F32)
        hs = sb("hs", [P, R, D], F32)
        hT = sb("hT", [P, C, N], F32)
        stats = sb("stats", [P, R, 6], F32)
        mv = sb("mv", [P, R, 2], F32)
        sd = sb("sd", [P, R], F32)
        rstd = sb("rstd", [P, R], F32)
        shift = sb("shift", [P, R], F32)
        adj_t = sb("adj_t", [P, N], I32)
        masks = sb("masks", [P, T1 + 1, N], U8)
        lhs = sb("lhs", [P, K0, C, P], F32)
        S = sb("S", [P, N], F32)
        tmp = sb("tmp", [P, N], F32)
        probs = sb("probs", [P, N], F32)
        pT = sb("pT", [P, R, P], F32)
        neg = sb("neg", [P, N], F32)
        nm = sb("nm", [P, 1], F32)
        rs = sb("rs", [P, 1], F32)
        rinv = sb("rinv", [P, 1], F32)
        hw = sb("hw", [P, R, WN], F32)
        hwt = sb("hwt", [P, WN], F32)
        eT = sb("eT", [2 * HT, N], F32)
        dst = sb("dst", [P, HT, N], F32)
        ot = sb("ot", [P, D], F32)
        hst = sb("hst", [P, H, 6], F32)
        hmv = sb("hmv", [P, H, 2], F32)
        hsd = sb("hsd", [P, H], F32)
        hrs = sb("hrs", [P, H], F32)
        ps_e = pb("ps_e", [P, 4, 512])
        ps_t = pb("ps_t", [P, 2, 512])
        ps_o = pb("ps_o", [P, 512])

        x_in, adj_in, masked = sem("x_in"), sem("adj_in"), sem("masked")
        stats_ready, sd_ready, norm_ready, h_ready = sem("stats_ready"), sem("sd_ready"), sem("norm_ready"), sem("h_ready")
        hT_psum, hT_ready = sem("hT_psum"), sem("hT_ready")
        ln_step, t0_step, t1_step = sem("ln_step"), sem("t0_step"), sem("t1_step")
        lhs_ready, e_ready, e_copied, e_used = sem("lhs_ready"), sem("e_ready"), sem("e_copied"), sem("e_used")
        m_ready, p_ready, pt_psum, pt_ready = sem("m_ready"), sem("p_ready"), sem("pt_psum"), sem("pt_ready")
        o_ready, o_used = sem("o_ready"), sem("o_used")
        proj_ready, proj_used, row_ready, row_used = sem("proj_ready"), sem("proj_used"), sem("row_ready"), sem("row_used")
        src_ready, z_ready, z_used = sem("src_ready"), sem("z_ready"), sem("z_used")
        m1_ready, p1_ready, pt1_psum, pt1_ready, o1_ready, o1_used = (
            sem(n) for n in ("m1_ready", "p1_ready", "pt1_psum", "pt1_ready", "o1_ready", "o1_used"))
        hst_ready, hsd_ready, out_ready, out_stored = sem("hst_ready"), sem("hsd_ready"), sem("out_ready"), sem("out_stored")
        idle = sb("idle", [P, 1], F32)
        neg_ready = sem("neg_ready")
        block = ctx.enter_context(nc.Block())

        def stand(signal, value):
            nc.vector.wait_ge(signal, value)
            nc.vector.memset(idle[:], 0.0)

        def guarded(eng, body):
            if flag is None:
                body()
            else:
                need = eng.value_load(flag, min_val=0, max_val=1)
                with eng.If(need > 0):
                    body()

        @block.sync
        def _(sp):
            def body():
                with sp.Fori(0, B) as b:
                    sp.wait_ge(out_stored, b * (16 * R) + 1)
                    sp.dma_start(xs[:], x[b, :, :].rearrange("(r p) d -> p r d", p=P)).then_inc(x_in, 16)
                    for layer in range(2):
                        with sp.Fori(0, R) as t:
                            sp.wait_ge(masked, b * (2 * R) + layer * R + t + 1)
                            sp.dma_start(adj_t[:], adj[b, bass.ts(t, P), :]).then_inc(adj_in, 16)
                            if layer:
                                sp.wait_ge(out_ready, b * R + t + 1)
                                sp.dma_start(out[b, bass.ts(t, P), :], ot[:]).then_inc(out_stored, 16)
                sp.wait_ge(out_stored, 16 * R * B + 1)
            guarded(sp, body)

        @block.tensor
        def _(pe):
            def transpose_h(n):
                pe.wait_ge(h_ready, n)
                for r in range(R):
                    for c in range(C):
                        last = pe.transpose(ps_e[:, 2 * c + r // 4, (r % 4) * P:(r % 4 + 1) * P],
                                            hs[:, r, c * P:(c + 1) * P], ident[:])
                last.then_inc(hT_psum, 1)

            def transpose_p():
                for j in range(R):
                    last = pe.transpose(ps_t[:, j // 4, (j % 4) * P:(j % 4 + 1) * P],
                                        probs[:, j * P:(j + 1) * P], ident[:])
                return last

            def body():
                with pe.Fori(0, B) as b:
                    transpose_h(b * 2 + 1)
                    with pe.Fori(0, R) as t:
                        n = b * R + t
                        pe.wait_ge(hT_ready, b * 2 + 1)
                        pe.wait_ge(lhs_ready, n + 1)
                        for q in range(K0):
                            pe.wait_ge(e_used, n * K0 + max(q - 1, 0) + 1)
                            for half in range(2):
                                for c in range(C):
                                    last = pe.matmul(ps_e[:, 2 * (q % 2) + half, :], lhs[:, q, c, :],
                                                     hT[:, c, half * 512:(half + 1) * 512],
                                                     start=(c == 0), stop=(c == C - 1))
                            last.then_inc(e_ready, 1)
                        pe.wait_ge(p_ready, n + 1)
                        transpose_p().then_inc(pt_psum, 1)
                        pe.wait_ge(pt_ready, n + 1)
                        for j in range(R):
                            last = pe.matmul(ps_o[:, 0:D], pT[:, j, :], hs[:, j, :],
                                             start=(j == 0), stop=(j == R - 1))
                        last.then_inc(o_ready, 1)
                    transpose_h(b * 2 + 2)
                    pe.wait_ge(hT_ready, b * 2 + 2)
                    for r in range(R):
                        if r >= 4:
                            pe.wait_ge(proj_used, b * R + r - 3)
                        for c in range(C):
                            last = pe.matmul(ps_e[:, r % 4, 0:WN], hT[:, c, r * P:(r + 1) * P], wa[:, c, :],
                                             start=(c == 0), stop=(c == C - 1))
                        last.then_inc(proj_ready, 1)
                    for half in range(2):
                        for c in range(C):
                            last = pe.matmul(ps_t[0:2 * HT, half, :], wa[:, c, D:WN],
                                             hT[:, c, half * 512:(half + 1) * 512],
                                             start=(c == 0), stop=(c == C - 1))
                    last.then_inc(row_ready, 1)
                    pe.wait_ge(row_used, b * (HT + 1) + 1)
                    pe.wait_ge(proj_used, b * R + R)
                    for r in range(HT):
                        if r >= 2:
                            pe.wait_ge(row_used, b * (HT + 1) + r)
                        for half in range(2):
                            last = pe.matmul(ps_e[:, 2 * (r % 2) + half, :], sel[:, r, :],
                                             eT[:, half * 512:(half + 1) * 512], start=True, stop=True)
                        last.then_inc(row_ready, 1)
                    with pe.Fori(0, R) as t:
                        for h in range(H):
                            n = b * (R * H) + t * H + h
                            pe.wait_ge(p1_ready, n + 1)
                            transpose_p().then_inc(pt1_psum, 1)
                            pe.wait_ge(pt1_ready, n + 1)
                            pe.wait_ge(o1_used, b * (R * H) + t * H + 1)
                            for j in range(R):
                                last = pe.matmul(ps_o[:, h * E:(h + 1) * E], pT[:, j, :],
                                                 hw[:, j, h * E:(h + 1) * E], start=(j == 0), stop=(j == R - 1))
                            last.then_inc(o1_ready, 1)
            guarded(pe, body)

        @block.scalar
        def _(act):
            def norm(n):
                act.wait_ge(stats_ready, n)
                act.activation(sd[:], mv[:, :, 1], ACT.Sqrt, bias=eps[:, 0:1]).then_inc(sd_ready, 1)
                act.wait_ge(norm_ready, n)
                for r in range(R):
                    last = act.activation(hs[:, r, :], xs[:, r, :], ACT.Relu,
                                          bias=shift[:, r:r + 1], scale=rstd[:, r:r + 1])
                last.then_inc(h_ready, 1)

            def body():
                with act.Fori(0, B) as b:
                    norm(b * 2 + 1)
                    with act.Fori(0, R) as t:
                        n = b * R + t
                        for q in range(K0):
                            act.wait_ge(e_ready, n * K0 + q + 1)
                            act.wait_ge(e_used, n * K0 + q + 1)
                            act.activation(tmp[:], ps_e[:, 2 * (q % 2):2 * (q % 2) + 2, :].rearrange("p a n -> p (a n)"),
                                           ACT.Copy).then_inc(e_copied, 1)
                        act.wait_ge(m_ready, n + 1)
                        act.activation(probs[:], S[:], ACT.Exp, bias=nm[:], accum_out=rs[:]).then_inc(p_ready, 1)
                        act.wait_ge(pt_psum, n + 1)
                        act.activation(pT[:].rearrange("p j i -> p (j i)"), ps_t[:].rearrange("p a n -> p (a n)"),
                                       ACT.Copy).then_inc(pt_ready, 1)
                    norm(b * 2 + 2)
                    act.wait_ge(row_ready, b * (HT + 1) + 1)
                    act.activation(eT[:], ps_t[0:2 * HT].rearrange("p a n -> p (a n)"), ACT.Copy).then_inc(row_used, 1)
                    for r in range(HT):
                        act.wait_ge(row_ready, b * (HT + 1) + r + 2)
                        act.activation(dst[:, r, :], ps_e[:, 2 * (r % 2):2 * (r % 2) + 2, :].rearrange("p a n -> p (a n)"),
                                       ACT.Copy).then_inc(row_used, 1)
                    act.wait_ge(row_used, b * (HT + 1) + HT + 1)
                    with act.Fori(0, R) as t:
                        act.wait_ge(src_ready, b * R + t + 1)
                        for h in range(H):
                            n = b * (R * H) + t * H + h
                            for q in range(T1):
                                act.wait_ge(z_used, n * T1 + q + 1)
                                col = D + h * T1 + q
                                act.activation(tmp[:], dst[:, h * T1 + q, :], ACT.Identity,
                                               bias=hwt[:, col:col + 1]).then_inc(z_ready, 1)
                            act.wait_ge(m1_ready, n + 1)
                            act.activation(probs[:], S[:], ACT.Exp, bias=nm[:], accum_out=rs[:]).then_inc(p1_ready, 1)
                            act.wait_ge(pt1_psum, n + 1)
                            act.activation(pT[:].rearrange("p j i -> p (j i)"), ps_t[:].rearrange("p a n -> p (a n)"),
                                           ACT.Copy).then_inc(pt1_ready, 1)
                        act.wait_ge(hst_ready, b * R + t + 1)
                        act.activation(hsd[:], hmv[:, :, 1], ACT.Sqrt, bias=eps[:, 1:2]).then_inc(hsd_ready, 1)
            guarded(act, body)

        LN_STEPS, T0_STEPS, T1_STEPS = 2, 3 + K0, 7 + 4 * H

        @block.vector
        def _(dve):
            def norm(n, first):
                s = Steps(dve, ln_step, first)
                for r in range(R):
                    last = dve.bn_stats(stats[:, r, :], xs[:, r, :])
                s.did(last)
                stand(s.sem, s.start + s.n)
                for r in range(R):
                    last = dve.bn_aggr(mv[:, r, :], stats[:, r, :])
                last.then_inc(stats_ready, 1)
                dve.wait_ge(sd_ready, n)
                s.did(dve.reciprocal(rstd[:], sd[:]))
                s.settle()
                dve.scalar_tensor_tensor(shift[:], mv[:, :, 0], -1.0, rstd[:], ALU.mult, ALU.mult).then_inc(norm_ready, 1)
                dve.wait_ge(hT_psum, n)
                for c in range(C):
                    last = dve.tensor_copy(hT[:, c, :], ps_e[:, 2 * c:2 * c + 2, :].rearrange("p a n -> p (a n)"))
                last.then_inc(hT_ready, 1)
                stand(hT_ready, n)
                assert s.n == LN_STEPS

            def body():
                for free in (masked, e_used, z_used, o1_used, out_stored):
                    dve.sem_inc(free, 1)
                dve.memset(neg[:], NEG1).then_inc(neg_ready, 1)
                dve.wait_ge(neg_ready, 1)
                with dve.Fori(0, B) as b:
                    dve.wait_ge(x_in, b * 16 + 16)
                    norm(b * 2 + 1, b * (2 * LN_STEPS))
                    with dve.Fori(0, R) as t:
                        n = b * R + t
                        s = Steps(dve, t0_step, n * T0_STEPS)
                        for q in range(K0):
                            for c in range(C):
                                last = dve.tensor_scalar(lhs[:, q, c, :], hT[:, c, bass.ts(t, P)],
                                                         aT[:, c, q:q + 1], None, ALU.mult)
                        last.then_inc(lhs_ready, 1)
                        dve.wait_ge(adj_in, b * (32 * R) + t * 16 + 16)
                        for q in range(K0):
                            last = dve.tensor_scalar(masks[:, q, :], adj_t[:], float(q + 1), None, ALU.is_equal)
                        last.then_inc(masked, 1)
                        s.did(dve.memset(S[:], NEG0))
                        s.settle()
                        dve.wait_ge(masked, b * (2 * R) + t + 1 + 1)
                        for q in range(K0):
                            dve.wait_ge(e_copied, n * K0 + q + 1)
                            s.did(dve.scalar_tensor_tensor(
                                tmp[:], ps_e[:, 2 * (q % 2):2 * (q % 2) + 2, :].rearrange("p a n -> p (a n)"),
                                SLOPE0, tmp[:], ALU.mult, ALU.max))
                            stand(s.sem, s.start + s.n)
                            dve.copy_predicated(S[:], masks[:, q, :], tmp[:]).then_inc(e_used, 1)
                        dve.wait_ge(e_used, n * K0 + K0 + 1)
                        dve.tensor_reduce(nm[:], S[:], AX_X, ALU.max, negate=True).then_inc(m_ready, 1)
                        dve.wait_ge(o_ready, n + 1)
                        s.did(dve.reciprocal(rinv[:], rs[:]))
                        s.settle()
                        s.did(dve.scalar_tensor_tensor(xs[:, bass.ts(t, 1), :].rearrange("p a d -> p (a d)"), ps_o[:, 0:D], rinv[:],
                                                       xs[:, bass.ts(t, 1), :].rearrange("p a d -> p (a d)"), ALU.mult, ALU.add))
                        s.settle()
                        assert s.n == T0_STEPS
                    norm(b * 2 + 2, b * (2 * LN_STEPS) + LN_STEPS)
                    for r in range(R):
                        dve.wait_ge(proj_ready, b * R + r + 1)
                        dve.tensor_copy(hw[:, r, :], ps_e[:, r % 4, 0:WN]).then_inc(proj_used, 1)
                    stand(proj_used, b * R + R)
                    with dve.Fori(0, R) as t:
                        n = b * R + t
                        s = Steps(dve, t1_step, n * T1_STEPS)
                        dve.tensor_copy(hwt[:], hw[:, bass.ts(t, 1), :].rearrange("p a d -> p (a d)")).then_inc(src_ready, 1)
                        dve.wait_ge(src_ready, n + 1)
                        dve.wait_ge(adj_in, b * (32 * R) + t * 16 + (16 * R + 16))
                        for q in range(T1 + 1):
                            last = dve.tensor_scalar(masks[:, q, :], adj_t[:], float(q), None, ALU.is_equal)
                        last.then_inc(masked, 1)
                        dve.wait_ge(masked, b * (2 * R) + t + (R + 1) + 1)
                        dve.wait_ge(out_stored, n * 16 + 1)
                        for h in range(H):
                            nh = n * H + h
                            s.did(dve.memset(S[:], 0.0))
                            for q in range(T1):
                                dve.wait_ge(z_ready, nh * T1 + q + 1)
                                stand(s.sem, s.start + s.n)
                                dve.copy_predicated(S[:], masks[:, q + 1, :], tmp[:]).then_inc(z_used, 1)
                                dve.wait_ge(z_used, nh * T1 + q + 1 + 1)
                            s.did(dve.scalar_tensor_tensor(S[:], S[:], SLOPE1, S[:], ALU.mult, ALU.max))
                            stand(s.sem, s.start + s.n)
                            s.did(dve.copy_predicated(S[:], masks[:, 0, :], neg[:]))
                            s.settle()
                            dve.tensor_reduce(nm[:], S[:], AX_X, ALU.max, negate=True).then_inc(m1_ready, 1)
                            dve.wait_ge(o1_ready, nh + 1)
                            s.did(dve.reciprocal(rinv[:], rs[:]))
                            s.settle()
                            dve.tensor_scalar(ot[:, h * E:(h + 1) * E], ps_o[:, h * E:(h + 1) * E], rinv[:], None,
                                              ALU.mult).then_inc(o1_used, 1)
                        dve.wait_ge(o1_used, n * H + H + 1)
                        s.did(dve.tensor_tensor(ot[:], ot[:], bgb[:, 0, :], ALU.add))
                        s.settle()
                        s.did(dve.scalar_tensor_tensor(ot[:], ot[:], 0.0, hwt[:, 0:D], ALU.max, ALU.add))
                        s.settle()
                        for h in range(H):
                            last = dve.bn_stats(hst[:, h, :], ot[:, h * E:(h + 1) * E])
                        s.did(last)
                        stand(s.sem, s.start + s.n)
                        for h in range(H):
                            last = dve.bn_aggr(hmv[:, h, :], hst[:, h, :])
                        last.then_inc(hst_ready, 1)
                        dve.wait_ge(hsd_ready, n + 1)
                        s.did(dve.reciprocal(hrs[:], hsd[:]))
                        s.settle()
                        for h in range(H):
                            last = dve.tensor_scalar(ot[:, h * E:(h + 1) * E], ot[:, h * E:(h + 1) * E],
                                                     hmv[:, h, 0:1], hrs[:, h:h + 1], ALU.subtract, ALU.mult)
                        s.did(last)
                        s.settle()
                        s.did(dve.tensor_tensor(ot[:], ot[:], bgb[:, 1, :], ALU.mult))
                        s.settle()
                        s.did(dve.tensor_tensor(ot[:], ot[:], bgb[:, 2, :], ALU.add))
                        s.settle()
                        dve.tensor_tensor(ot[:], ot[:], xs[:, bass.ts(t, 1), :].rearrange("p a d -> p (a d)"), ALU.add).then_inc(out_ready, 1)
                        assert s.n == T1_STEPS
            guarded(dve, body)


def program(nc, ins, out):
    with ExitStack() as ctx:
        k = constants(nc, ctx, ins)
        general_path(nc, k, ins, out, None)


_INS = ["x", "adj", "L0_gnn_a_0", "L0_gnn_a_1", "L0_gnn_a_2", "L0_gnn_a_3", "L1_gnn_W", "L1_gnn_a_src",
        "L1_gnn_a_dst", "L1_gnn_bias", "L1_gnn_ln_gamma", "L1_gnn_ln_beta"]


def kernel(**inputs):
    import numpy as _np
    import concourse.bacc as _bacc
    from concourse import mybir as _mybir
    from concourse.bass_utils import run_bass_kernel_spmd as _run

    nc = _bacc.Bacc("TRN2", target_bir_lowering=False, num_devices=1)
    arrays, aps = {}, {}
    for name in _INS:
        a = _np.ascontiguousarray(inputs[name])
        arrays[f"in_{name}"] = a
        aps[name] = nc.dram_tensor(f"in_{name}", a.shape, _mybir.dt.from_np(a.dtype), kind="ExternalInput").ap()
    out = nc.dram_tensor("out_0", (B, N, D), F32, kind="ExternalOutput").ap()
    program(nc, aps, out)
    r = _run(nc, [arrays], core_ids=[0])
    return r.results[0]["out_0"]
```

```python
from contextlib import ExitStack
from itertools import count

import concourse.bass as bass
from concourse import mybir

ALU = mybir.AluOpType
ACT = mybir.ActivationFunctionType
F32 = mybir.dt.float32
BF16 = mybir.dt.bfloat16
I32 = mybir.dt.int32
U8 = mybir.dt.uint8
U32 = mybir.dt.uint32
AX_X = mybir.AxisListType.X

P = 128
B, N, D = 16, 1024, 256
R = N // P
C = D // P
K0 = 4
H, E, T1 = 4, 64, 5
HT = H * T1
WN = D + 2 * HT
WF = D + 2 * H
LN_EPS = 1e-5
HEAD_EPS = 1e-6
SLOPE0, SLOPE1 = 0.2, 0.01
NEG0, NEG1 = -9000000000000000.0, -1000000000.0
BIG = 2.0 ** 90
SPREAD = 40.0
CAP = 44.0
UNITS = R * H
Q_RING = 4
ADJ_RING = 2
TINY = 2.0 ** -100
LIMIT = 2.0 ** 80
UNIT_PLAN = [(0, 0)] * 4 + [(0, 8), (4, 4), (4, 4), (4, 0)]
END_PLAN = (2, 2)


class Steps:

    def __init__(self, eng, sem, start=0):
        self.eng, self.sem, self.start, self.n = eng, sem, start, 0

    def did(self, ins):
        ins.then_inc(self.sem, 1)
        self.n += 1

    def settle(self):
        self.eng.wait_ge(self.sem, self.start + self.n)


def constants(nc, ctx, ins):
    sb = lambda name, shape, dt: ctx.enter_context(nc.sbuf_tensor(name, shape, dt))
    sem = lambda name: ctx.enter_context(nc.semaphore(name))
    k = {
        "ident": sb("ident", [P, P], F32),
        "aT": sb("aT", [P, C, K0], F32),
        "wa": sb("wa", [P, C, WN], F32),
        "bgb": sb("bgb", [P, 3, D], F32),
        "eps": sb("eps", [P, 2], F32),
        "identb": sb("identb", [P, P], BF16),
        "one": sb("one", [P, 1], F32),
        "half": sb("half", [P, R * H], F32),
        "pick": sb("pick", [3 * H, H, P], BF16),
        "wf": sb("wf", [P, C, WF], F32),
    }
    identb, one, half, pick, wf = (k[n] for n in ("identb", "one", "half", "pick", "wf"))
    ident, aT, wa, bgb, eps = (k[n] for n in ("ident", "aT", "wa", "bgb", "eps"))
    with ExitStack() as own:
        tb = lambda name, shape, dt: own.enter_context(nc.sbuf_tensor(name, shape, dt))
        pb = lambda name, shape: own.enter_context(nc.psum_tensor(name, shape, F32))
        sm = lambda name: own.enter_context(nc.semaphore(name))
        attn_rows = tb("attn_rows", [2 * HT, E], F32)
        attn_cols = tb("attn_cols", [E, 2 * HT], F32)
        wT = tb("wT", [E, H, D], F32)
        rows = tb("rows", [1, 3, D], F32)
        ones = tb("ones", [1, P], F32)
        ps_wT = pb("ps_wT", [P, 2, 512])
        ps_wa = pb("ps_wa", [P, C, 2 * HT])
        ps_rows = pb("ps_rows", [P, 2, 512])
        ps_at = pb("ps_at", [P, 512])
        w_in, rows_in, attn_in = sm("w_in"), sm("rows_in"), sm("attn_in")
        filled, ident_ready, turned, turned_out, folded, spread = (
            sm(n) for n in ("filled", "ident_ready", "turned", "turned_out", "folded", "spread"))
        block = own.enter_context(nc.Block())

        @block.sync
        def _(sp):
            for h in range(H):
                sp.dma_start(wa[:, :, h * E:(h + 1) * E],
                             ins["L1_gnn_W"][h].rearrange("(c p) e -> p c e", p=P)).then_inc(w_in, 16)
            for k_, name in enumerate(["L0_gnn_a_0", "L0_gnn_a_1", "L0_gnn_a_2", "L0_gnn_a_3"]):
                sp.dma_start(aT[:, :, k_:k_ + 1],
                             ins[name].rearrange("(c p) o -> p c o", p=P),
                             allow_slow_non_contiguous=True).then_inc(w_in, 16)
            sp.wait_ge(w_in, 16 * (H + K0))

        @block.scalar
        def _(act):
            for i, name in enumerate(["L1_gnn_a_src", "L1_gnn_a_dst"]):
                act.dma_start(attn_rows[i * HT:(i + 1) * HT, :],
                              ins[name].rearrange("h t e -> (h t) e")).then_inc(attn_in, 16)
            for i, name in enumerate(["L1_gnn_bias", "L1_gnn_ln_gamma", "L1_gnn_ln_beta"]):
                act.dma_start(rows[:, i, :], ins[name].rearrange("(o h) e -> o (h e)", o=1)).then_inc(rows_in, 16)
            act.wait_ge(rows_in, 48)

        @block.gpsimd
        def _(pool):
            pool.memset(ident[:], 0.0).then_inc(filled, 1)
            pool.memset(ones[:], 1.0).then_inc(filled, 1)
            pool.memset(eps[:, 0:1], LN_EPS).then_inc(filled, 1)
            pool.memset(eps[:, 1:2], HEAD_EPS).then_inc(filled, 1)
            pool.memset(one[:], 1.0).then_inc(filled, 1)
            pool.memset(half[:], -0.5).then_inc(filled, 1)
            pool.memset(pick[:], 0.0).then_inc(filled, 1)
            pool.wait_ge(filled, 7)
            pool.affine_select(out=ident[:], in_=ident[:], compare_op=ALU.not_equal, fill=1.0, base=0,
                               pattern=[[-1, P]], channel_multiplier=1).then_inc(ident_ready, 1)
            pool.wait_ge(ident_ready, 1)
            pool.tensor_copy(identb[:], ident[:]).then_inc(ident_ready, 1)
            for part in range(3):
                pool.affine_select(out=pick[:], in_=pick[:], compare_op=ALU.not_equal, fill=1.0, base=-part * H,
                                   pattern=[[-1, H], [0, P]], channel_multiplier=1).then_inc(ident_ready, 1)
                pool.wait_ge(ident_ready, 3 + part)

        @block.tensor
        def _(pe):
            pe.wait_ge(ident_ready, 1)
            pe.wait_ge(w_in, 16 * (H + K0))
            pe.wait_ge(attn_in, 32)
            for h in range(H):
                for c in range(C):
                    last = pe.transpose(ps_wT[0:E, h // 2, (h % 2) * D + c * P:(h % 2) * D + (c + 1) * P],
                                        wa[:, c, h * E:(h + 1) * E], ident[:])
            last = pe.transpose(ps_at[0:E, 0:2 * HT], attn_rows[:], ident[0:2 * HT, 0:2 * HT])
            last.then_inc(turned, 1)
            pe.wait_ge(rows_in, 48)
            pe.wait_ge(filled, 7)
            flat = rows[:, :, :].rearrange("p a d -> p (a d)")
            pe.matmul(ps_rows[:, 0, :], ones[:], flat[:, 0:512], start=True, stop=True)
            pe.matmul(ps_rows[:, 1, 0:D], ones[:], flat[:, 512:768], start=True, stop=True).then_inc(spread, 1)
            pe.wait_ge(turned_out, 2)
            for c in range(C):
                for h in range(H):
                    for s in range(2):
                        col = s * HT + h * T1
                        last = pe.matmul(ps_wa[:, c, col:col + T1], wT[:, h, c * P:(c + 1) * P],
                                         attn_cols[:, col:col + T1], start=True, stop=True)
            last.then_inc(folded, 1)

        @block.vector
        def _(dve):
            dve.wait_ge(turned, 1)
            dve.tensor_copy(wT[:].rearrange("p (a b) d -> p a (b d)", a=2), ps_wT[0:E, :, :]).then_inc(turned_out, 1)
            dve.tensor_copy(attn_cols[:], ps_at[0:E, 0:2 * HT]).then_inc(turned_out, 1)
            dve.wait_ge(spread, 1)
            flat = bgb[:].rearrange("p a d -> p (a d)")
            dve.tensor_copy(flat[:, 0:512], ps_rows[:, 0, :])
            dve.tensor_copy(flat[:, 512:768], ps_rows[:, 1, 0:D])
            dve.wait_ge(folded, 1)
            dve.tensor_copy(wa[:, :, D:WN], ps_wa[:]).then_inc(folded, 1)
            dve.wait_ge(folded, 2)
            dve.tensor_copy(wf[:, :, 0:D], wa[:, :, 0:D])
            for s in range(2):
                dve.tensor_copy(wf[:, :, D + s * H:D + (s + 1) * H],
                                wa[:, :, D + s * HT:D + (s + 1) * HT].rearrange("p c (h t) -> p c h t", h=H)[:, :, :, 0])
    return k


def general_path(nc, k, ins, out, flag):
    x, adj = ins["x"], ins["adj"]
    ident, aT, wa, bgb, eps = (k[n] for n in ("ident", "aT", "wa", "bgb", "eps"))
    with ExitStack() as ctx:
        sb = lambda name, shape, dt: ctx.enter_context(nc.sbuf_tensor("g_" + name, shape, dt))
        pb = lambda name, shape: ctx.enter_context(nc.psum_tensor("g_" + name, shape, F32))
        sem = lambda name: ctx.enter_context(nc.semaphore("g_" + name))
        xs = sb("xs", [P, R, D], F32)
        hs = sb("hs", [P, R, D], F32)
        hT = sb("hT", [P, C, N], F32)
        stats = sb("stats", [P, R, 6], F32)
        mv = sb("mv", [P, R, 2], F32)
        sd = sb("sd", [P, R], F32)
        rstd = sb("rstd", [P, R], F32)
        shift = sb("shift", [P, R], F32)
        adj_t = sb("adj_t", [P, N], I32)
        masks = sb("masks", [P, T1 + 1, N], U8)
        lhs = sb("lhs", [P, K0, C, P], F32)
        S = sb("S", [P, N], F32)
        tmp = sb("tmp", [P, N], F32)
        probs = sb("probs", [P, N], F32)
        pT = sb("pT", [P, R, P], F32)
        neg = sb("neg", [P, N], F32)
        nm = sb("nm", [P, 1], F32)
        rs = sb("rs", [P, 1], F32)
        rinv = sb("rinv", [P, 1], F32)
        hw = sb("hw", [P, R, WN], F32)
        hwt = sb("hwt", [P, WN], F32)
        eT = sb("eT", [2 * HT, N], F32)
        dst = sb("dst", [P, HT, N], F32)
        ot = sb("ot", [P, D], F32)
        hst = sb("hst", [P, H, 6], F32)
        hmv = sb("hmv", [P, H, 2], F32)
        hsd = sb("hsd", [P, H], F32)
        hrs = sb("hrs", [P, H], F32)
        ps_e = pb("ps_e", [P, 4, 512])
        ps_t = pb("ps_t", [P, 2, 512])
        ps_o = pb("ps_o", [P, 512])

        x_in, adj_in, masked = sem("x_in"), sem("adj_in"), sem("masked")
        stats_ready, sd_ready, norm_ready, h_ready = sem("stats_ready"), sem("sd_ready"), sem("norm_ready"), sem("h_ready")
        hT_psum, hT_ready = sem("hT_psum"), sem("hT_ready")
        ln_step, t0_step, t1_step = sem("ln_step"), sem("t0_step"), sem("t1_step")
        lhs_ready, e_ready, e_copied, e_used = sem("lhs_ready"), sem("e_ready"), sem("e_copied"), sem("e_used")
        m_ready, p_ready, pt_psum, pt_ready = sem("m_ready"), sem("p_ready"), sem("pt_psum"), sem("pt_ready")
        o_ready, o_used = sem("o_ready"), sem("o_used")
        proj_ready, proj_used, row_ready, row_used = sem("proj_ready"), sem("proj_used"), sem("row_ready"), sem("row_used")
        src_ready, z_ready, z_used = sem("src_ready"), sem("z_ready"), sem("z_used")
        m1_ready, p1_ready, pt1_psum, pt1_ready, o1_ready, o1_used = (
            sem(n) for n in ("m1_ready", "p1_ready", "pt1_psum", "pt1_ready", "o1_ready", "o1_used"))
        hst_ready, hsd_ready, out_ready, out_stored = sem("hst_ready"), sem("hsd_ready"), sem("out_ready"), sem("out_stored")
        sel = sb("sel", [2 * HT, HT, P], F32)
        idle = sb("idle", [P, 1], F32)
        sel_zero, sel_ready = sem("sel_zero"), sem("sel_ready")
        neg_ready = sem("neg_ready")
        block = ctx.enter_context(nc.Block())

        def stand(signal, value):
            nc.vector.wait_ge(signal, value)
            nc.vector.memset(idle[:], 0.0)

        def guarded(eng, body):
            if flag is None:
                body()
            else:
                need = eng.value_load(flag, min_val=0, max_val=1)
                with eng.If(need > 0):
                    body()

        @block.sync
        def _(sp):
            def body():
                with sp.Fori(0, B) as b:
                    sp.wait_ge(out_stored, b * (16 * R) + 1)
                    sp.dma_start(xs[:], x[b, :, :].rearrange("(r p) d -> p r d", p=P)).then_inc(x_in, 16)
                    for layer in range(2):
                        with sp.Fori(0, R) as t:
                            sp.wait_ge(masked, b * (2 * R) + layer * R + t + 1)
                            sp.dma_start(adj_t[:], adj[b, bass.ts(t, P), :]).then_inc(adj_in, 16)
                            if layer:
                                sp.wait_ge(out_ready, b * R + t + 1)
                                sp.dma_start(out[b, bass.ts(t, P), :], ot[:]).then_inc(out_stored, 16)
                sp.wait_ge(out_stored, 16 * R * B + 1)
            guarded(sp, body)

        @block.gpsimd
        def _(pool):
            def body():
                pool.memset(sel[:], 0.0).then_inc(sel_zero, 1)
                pool.wait_ge(sel_zero, 1)
                pool.affine_select(out=sel[:], in_=sel[:], compare_op=ALU.not_equal, fill=1.0, base=-HT,
                                   pattern=[[-1, HT], [0, P]], channel_multiplier=1).then_inc(sel_ready, 1)
            guarded(pool, body)

        @block.tensor
        def _(pe):
            def transpose_h(n):
                pe.wait_ge(h_ready, n)
                for r in range(R):
                    for c in range(C):
                        last = pe.transpose(ps_e[:, 2 * c + r // 4, (r % 4) * P:(r % 4 + 1) * P],
                                            hs[:, r, c * P:(c + 1) * P], ident[:])
                last.then_inc(hT_psum, 1)

            def transpose_p():
                for j in range(R):
                    last = pe.transpose(ps_t[:, j // 4, (j % 4) * P:(j % 4 + 1) * P],
                                        probs[:, j * P:(j + 1) * P], ident[:])
                return last

            def body():
                pe.wait_ge(sel_ready, 1)
                with pe.Fori(0, B) as b:
                    transpose_h(b * 2 + 1)
                    with pe.Fori(0, R) as t:
                        n = b * R + t
                        pe.wait_ge(hT_ready, b * 2 + 1)
                        pe.wait_ge(lhs_ready, n + 1)
                        for q in range(K0):
                            pe.wait_ge(e_used, n * K0 + max(q - 1, 0) + 1)
                            for half in range(2):
                                for c in range(C):
                                    last = pe.matmul(ps_e[:, 2 * (q % 2) + half, :], lhs[:, q, c, :],
                                                     hT[:, c, half * 512:(half + 1) * 512],
                                                     start=(c == 0), stop=(c == C - 1))
                            last.then_inc(e_ready, 1)
                        pe.wait_ge(p_ready, n + 1)
                        transpose_p().then_inc(pt_psum, 1)
                        pe.wait_ge(pt_ready, n + 1)
                        for j in range(R):
                            last = pe.matmul(ps_o[:, 0:D], pT[:, j, :], hs[:, j, :],
                                             start=(j == 0), stop=(j == R - 1))
                        last.then_inc(o_ready, 1)
                    transpose_h(b * 2 + 2)
                    pe.wait_ge(hT_ready, b * 2 + 2)
                    for r in range(R):
                        if r >= 4:
                            pe.wait_ge(proj_used, b * R + r - 3)
                        for c in range(C):
                            last = pe.matmul(ps_e[:, r % 4, 0:WN], hT[:, c, r * P:(r + 1) * P], wa[:, c, :],
                                             start=(c == 0), stop=(c == C - 1))
                        last.then_inc(proj_ready, 1)
                    for half in range(2):
                        for c in range(C):
                            last = pe.matmul(ps_t[0:2 * HT, half, :], wa[:, c, D:WN],
                                             hT[:, c, half * 512:(half + 1) * 512],
                                             start=(c == 0), stop=(c == C - 1))
                    last.then_inc(row_ready, 1)
                    pe.wait_ge(row_used, b * (HT + 1) + 1)
                    pe.wait_ge(proj_used, b * R + R)
                    for r in range(HT):
                        if r >= 2:
                            pe.wait_ge(row_used, b * (HT + 1) + r)
                        for half in range(2):
                            last = pe.matmul(ps_e[:, 2 * (r % 2) + half, :], sel[:, r, :],
                                             eT[:, half * 512:(half + 1) * 512], start=True, stop=True)
                        last.then_inc(row_ready, 1)
                    with pe.Fori(0, R) as t:
                        for h in range(H):
                            n = b * (R * H) + t * H + h
                            pe.wait_ge(p1_ready, n + 1)
                            transpose_p().then_inc(pt1_psum, 1)
                            pe.wait_ge(pt1_ready, n + 1)
                            pe.wait_ge(o1_used, b * (R * H) + t * H + 1)
                            for j in range(R):
                                last = pe.matmul(ps_o[:, h * E:(h + 1) * E], pT[:, j, :],
                                                 hw[:, j, h * E:(h + 1) * E], start=(j == 0), stop=(j == R - 1))
                            last.then_inc(o1_ready, 1)
            guarded(pe, body)

        @block.scalar
        def _(act):
            def norm(n):
                act.wait_ge(stats_ready, n)
                act.activation(sd[:], mv[:, :, 1], ACT.Sqrt, bias=eps[:, 0:1]).then_inc(sd_ready, 1)
                act.wait_ge(norm_ready, n)
                for r in range(R):
                    last = act.activation(hs[:, r, :], xs[:, r, :], ACT.Relu,
                                          bias=shift[:, r:r + 1], scale=rstd[:, r:r + 1])
                last.then_inc(h_ready, 1)

            def body():
                with act.Fori(0, B) as b:
                    norm(b * 2 + 1)
                    with act.Fori(0, R) as t:
                        n = b * R + t
                        for q in range(K0):
                            act.wait_ge(e_ready, n * K0 + q + 1)
                            act.wait_ge(e_used, n * K0 + q + 1)
                            act.activation(tmp[:], ps_e[:, 2 * (q % 2):2 * (q % 2) + 2, :].rearrange("p a n -> p (a n)"),
                                           ACT.Copy).then_inc(e_copied, 1)
                        act.wait_ge(m_ready, n + 1)
                        act.activation(probs[:], S[:], ACT.Exp, bias=nm[:], accum_out=rs[:]).then_inc(p_ready, 1)
                        act.wait_ge(pt_psum, n + 1)
                        act.activation(pT[:].rearrange("p j i -> p (j i)"), ps_t[:].rearrange("p a n -> p (a n)"),
                                       ACT.Copy).then_inc(pt_ready, 1)
                    norm(b * 2 + 2)
                    act.wait_ge(row_ready, b * (HT + 1) + 1)
                    act.activation(eT[:], ps_t[0:2 * HT].rearrange("p a n -> p (a n)"), ACT.Copy).then_inc(row_used, 1)
                    for r in range(HT):
                        act.wait_ge(row_ready, b * (HT + 1) + r + 2)
                        act.activation(dst[:, r, :], ps_e[:, 2 * (r % 2):2 * (r % 2) + 2, :].rearrange("p a n -> p (a n)"),
                                       ACT.Copy).then_inc(row_used, 1)
                    act.wait_ge(row_used, b * (HT + 1) + HT + 1)
                    with act.Fori(0, R) as t:
                        act.wait_ge(src_ready, b * R + t + 1)
                        for h in range(H):
                            n = b * (R * H) + t * H + h
                            for q in range(T1):
                                act.wait_ge(z_used, n * T1 + q + 1)
                                col = D + h * T1 + q
                                act.activation(tmp[:], dst[:, h * T1 + q, :], ACT.Identity,
                                               bias=hwt[:, col:col + 1]).then_inc(z_ready, 1)
                            act.wait_ge(m1_ready, n + 1)
                            act.activation(probs[:], S[:], ACT.Exp, bias=nm[:], accum_out=rs[:]).then_inc(p1_ready, 1)
                            act.wait_ge(pt1_psum, n + 1)
                            act.activation(pT[:].rearrange("p j i -> p (j i)"), ps_t[:].rearrange("p a n -> p (a n)"),
                                           ACT.Copy).then_inc(pt1_ready, 1)
                        act.wait_ge(hst_ready, b * R + t + 1)
                        act.activation(hsd[:], hmv[:, :, 1], ACT.Sqrt, bias=eps[:, 1:2]).then_inc(hsd_ready, 1)
            guarded(act, body)

        LN_STEPS, T0_STEPS, T1_STEPS = 2, 3 + K0, 7 + 4 * H

        @block.vector
        def _(dve):
            def norm(n, first):
                s = Steps(dve, ln_step, first)
                for r in range(R):
                    last = dve.bn_stats(stats[:, r, :], xs[:, r, :])
                s.did(last)
                stand(s.sem, s.start + s.n)
                for r in range(R):
                    last = dve.bn_aggr(mv[:, r, :], stats[:, r, :])
                last.then_inc(stats_ready, 1)
                dve.wait_ge(sd_ready, n)
                s.did(dve.reciprocal(rstd[:], sd[:]))
                s.settle()
                dve.scalar_tensor_tensor(shift[:], mv[:, :, 0], -1.0, rstd[:], ALU.mult, ALU.mult).then_inc(norm_ready, 1)
                dve.wait_ge(hT_psum, n)
                for c in range(C):
                    last = dve.tensor_copy(hT[:, c, :], ps_e[:, 2 * c:2 * c + 2, :].rearrange("p a n -> p (a n)"))
                last.then_inc(hT_ready, 1)
                stand(hT_ready, n)
                assert s.n == LN_STEPS

            def body():
                for free in (masked, e_used, z_used, o1_used, out_stored):
                    dve.sem_inc(free, 1)
                dve.memset(neg[:], NEG1).then_inc(neg_ready, 1)
                dve.wait_ge(neg_ready, 1)
                with dve.Fori(0, B) as b:
                    dve.wait_ge(x_in, b * 16 + 16)
                    norm(b * 2 + 1, b * (2 * LN_STEPS))
                    with dve.Fori(0, R) as t:
                        n = b * R + t
                        s = Steps(dve, t0_step, n * T0_STEPS)
                        for q in range(K0):
                            for c in range(C):
                                last = dve.tensor_scalar(lhs[:, q, c, :], hT[:, c, bass.ts(t, P)],
                                                         aT[:, c, q:q + 1], None, ALU.mult)
                        last.then_inc(lhs_ready, 1)
                        dve.wait_ge(adj_in, b * (32 * R) + t * 16 + 16)
                        for q in range(K0):
                            last = dve.tensor_scalar(masks[:, q, :], adj_t[:], float(q + 1), None, ALU.is_equal)
                        last.then_inc(masked, 1)
                        s.did(dve.memset(S[:], NEG0))
                        s.settle()
                        dve.wait_ge(masked, b * (2 * R) + t + 1 + 1)
                        for q in range(K0):
                            dve.wait_ge(e_copied, n * K0 + q + 1)
                            s.did(dve.scalar_tensor_tensor(
                                tmp[:], ps_e[:, 2 * (q % 2):2 * (q % 2) + 2, :].rearrange("p a n -> p (a n)"),
                                SLOPE0, tmp[:], ALU.mult, ALU.max))
                            stand(s.sem, s.start + s.n)
                            dve.copy_predicated(S[:], masks[:, q, :], tmp[:]).then_inc(e_used, 1)
                        dve.wait_ge(e_used, n * K0 + K0 + 1)
                        dve.tensor_reduce(nm[:], S[:], AX_X, ALU.max, negate=True).then_inc(m_ready, 1)
                        dve.wait_ge(o_ready, n + 1)
                        s.did(dve.reciprocal(rinv[:], rs[:]))
                        s.settle()
                        s.did(dve.scalar_tensor_tensor(xs[:, bass.ts(t, 1), :].rearrange("p a d -> p (a d)"), ps_o[:, 0:D], rinv[:],
                                                       xs[:, bass.ts(t, 1), :].rearrange("p a d -> p (a d)"), ALU.mult, ALU.add))
                        s.settle()
                        assert s.n == T0_STEPS
                    norm(b * 2 + 2, b * (2 * LN_STEPS) + LN_STEPS)
                    for r in range(R):
                        dve.wait_ge(proj_ready, b * R + r + 1)
                        dve.tensor_copy(hw[:, r, :], ps_e[:, r % 4, 0:WN]).then_inc(proj_used, 1)
                    stand(proj_used, b * R + R)
                    with dve.Fori(0, R) as t:
                        n = b * R + t
                        s = Steps(dve, t1_step, n * T1_STEPS)
                        dve.tensor_copy(hwt[:], hw[:, bass.ts(t, 1), :].rearrange("p a d -> p (a d)")).then_inc(src_ready, 1)
                        dve.wait_ge(src_ready, n + 1)
                        dve.wait_ge(adj_in, b * (32 * R) + t * 16 + (16 * R + 16))
                        for q in range(T1 + 1):
                            last = dve.tensor_scalar(masks[:, q, :], adj_t[:], float(q), None, ALU.is_equal)
                        last.then_inc(masked, 1)
                        dve.wait_ge(masked, b * (2 * R) + t + (R + 1) + 1)
                        dve.wait_ge(out_stored, n * 16 + 1)
                        for h in range(H):
                            nh = n * H + h
                            s.did(dve.memset(S[:], 0.0))
                            for q in range(T1):
                                dve.wait_ge(z_ready, nh * T1 + q + 1)
                                stand(s.sem, s.start + s.n)
                                dve.copy_predicated(S[:], masks[:, q + 1, :], tmp[:]).then_inc(z_used, 1)
                                dve.wait_ge(z_used, nh * T1 + q + 1 + 1)
                            s.did(dve.scalar_tensor_tensor(S[:], S[:], SLOPE1, S[:], ALU.mult, ALU.max))
                            stand(s.sem, s.start + s.n)
                            s.did(dve.copy_predicated(S[:], masks[:, 0, :], neg[:]))
                            s.settle()
                            dve.tensor_reduce(nm[:], S[:], AX_X, ALU.max, negate=True).then_inc(m1_ready, 1)
                            dve.wait_ge(o1_ready, nh + 1)
                            s.did(dve.reciprocal(rinv[:], rs[:]))
                            s.settle()
                            dve.tensor_scalar(ot[:, h * E:(h + 1) * E], ps_o[:, h * E:(h + 1) * E], rinv[:], None,
                                              ALU.mult).then_inc(o1_used, 1)
                        dve.wait_ge(o1_used, n * H + H + 1)
                        s.did(dve.tensor_tensor(ot[:], ot[:], bgb[:, 0, :], ALU.add))
                        s.settle()
                        s.did(dve.scalar_tensor_tensor(ot[:], ot[:], 0.0, hwt[:, 0:D], ALU.max, ALU.add))
                        s.settle()
                        for h in range(H):
                            last = dve.bn_stats(hst[:, h, :], ot[:, h * E:(h + 1) * E])
                        s.did(last)
                        stand(s.sem, s.start + s.n)
                        for h in range(H):
                            last = dve.bn_aggr(hmv[:, h, :], hst[:, h, :])
                        last.then_inc(hst_ready, 1)
                        dve.wait_ge(hsd_ready, n + 1)
                        s.did(dve.reciprocal(hrs[:], hsd[:]))
                        s.settle()
                        for h in range(H):
                            last = dve.tensor_scalar(ot[:, h * E:(h + 1) * E], ot[:, h * E:(h + 1) * E],
                                                     hmv[:, h, 0:1], hrs[:, h:h + 1], ALU.subtract, ALU.mult)
                        s.did(last)
                        s.settle()
                        s.did(dve.tensor_tensor(ot[:], ot[:], bgb[:, 1, :], ALU.mult))
                        s.settle()
                        s.did(dve.tensor_tensor(ot[:], ot[:], bgb[:, 2, :], ALU.add))
                        s.settle()
                        dve.tensor_tensor(ot[:], ot[:], xs[:, bass.ts(t, 1), :].rearrange("p a d -> p (a d)"), ALU.add).then_inc(out_ready, 1)
                        assert s.n == T1_STEPS
            guarded(dve, body)


def need(eng, signal, value):
    if not isinstance(value, int) or value > 0:
        eng.wait_ge(signal, value)


def plain_path(nc, k, ins, out, flag):
    x, adj = ins["x"], ins["adj"]
    ident, identb, aT, wf, bgb, eps, one, half, pick = (
        k[n] for n in ("ident", "identb", "aT", "wf", "bgb", "eps", "one", "half", "pick"))
    with ExitStack() as ctx:
        sb = lambda name, shape, dt=F32: ctx.enter_context(nc.sbuf_tensor("f_" + name, shape, dt))
        pb = lambda name, shape, dt=F32: ctx.enter_context(nc.psum_tensor("f_" + name, shape, dt))
        xs = [sb(f"xs{i}", [P, R, D]) for i in range(2)]
        hs = [sb(f"hs{i}", [P, R, D]) for i in range(2)]
        hT = sb("hT", [P, C, N])
        ahT = sb("ahT", [P, C, N])
        adj_t = [sb(f"adj{i}", [P, N], I32) for i in range(ADJ_RING)]
        off = [sb(f"off{i}", [P, N], BF16) for i in range(ADJ_RING)]
        mT = [sb(f"mT{i}", [P, R, N], BF16) for i in range(2)]
        pos = sb("pos", [P, N])
        ps = [sb(f"ps{i}", [P, N]) for i in range(2)]
        rs = [sb(f"rs{i}", [P, 1]) for i in range(2)]
        rinv = sb("rinv", [P, 1])
        nm = sb("nm", [P, R])
        pT = sb("pT", [P, R, P])
        stats0, mv0, var0, rstd0, shift0 = sb("stats0", [P, R, 6]), sb("mv0", [P, R, 2]), sb("var0", [P, R]), sb("rstd0", [P, R]), sb("shift0", [P, R])
        stats1, mv1, var1, rstd1, shift1 = sb("stats1", [P, R, 6]), sb("mv1", [P, R, 2]), sb("var1", [P, R]), sb("rstd1", [P, R]), sb("shift1", [P, R])
        h1 = sb("h1", [P, R, D])
        h1T = sb("h1T", [P, C, N])
        hw = sb("hw", [P, R, WF])
        hb = sb("hb", [P, R, H, E + 1])
        ends = sb("ends", [P, 2 * H])
        all_ends = sb("all_ends", [P, 2 * H])
        argd, argb, argu, argc = sb("argd", [P, R, H]), sb("argb", [P, R, H]), sb("argu", [P, R, H]), sb("argc", [P, R, H])
        V, U, rest = sb("V", [P, R, H]), sb("U", [P, R, H]), sb("rest", [P, 2, R, H])
        parts = sb("parts", [P, R, 3, H], BF16)
        uT = sb("uT", [3 * H, N], BF16)
        ub = [sb(f"ub{h}", [P, N]) for h in range(H)]
        qs = [sb(f"qs{i}", [P, N]) for i in range(Q_RING)]
        nT = h1T[0:E + 1, 0, :]
        nsum, ninv = sb("nsum", [P, R]), sb("ninv", [P, R])
        y = sb("y", [P, R, D])
        hst = sb("hst", [P, R * H, 6])
        hsum, hdif, hm2, hsq, hvar, hve, hrstd = (sb(n, [P, R * H]) for n in ("hsum", "hdif", "hm2", "hsq", "hvar", "hve", "hrstd"))
        xb = sb("xb", [P, R, D])
        idle = sb("idle", [P, 16])
        idle_p = sb("idle_p", [P, 16])
        turns = count()
        worst = sb("worst", [P, B])
        spread = sb("spread", [P, B, H])
        good = sb("good", [P, B * (H + 1)])
        bad = sb("bad", [P, 2])
        e_ps = pb("e_ps", [P, 2, 512])
        t_ps = pb("t_ps", [P, 2, 512])
        o_ps = pb("o_ps", [P, 512])
        m_ps = pb("m_ps", [P, N], BF16)
        n_ps = pb("n_ps", [P, 2, 512])
        flat = lambda a: a.rearrange("p a n -> p (a n)")
        num = lambda: t_ps[:, :, 0:4 * (E + 1)].rearrange("p a (r e) -> p a r e", r=4)

        S = {n: ctx.enter_context(nc.semaphore("f_" + n)) for n in (
            "x_in adj0_in adj1_in out_stored "
            "e_ready mt_psum pt_psum o_ready hT_psum h1T_psum pj_ready ut_psum ub_psum unit_done head_psum "
            "pos_ready mt_ready p_ready pt_ready h0_ready h1_ready hT_ready h1T_ready hw_ready ex_ready ut_ready ub_ready nT_ready "
            "t_ready x1_ready x1_step ln1_step st0_ready st1_ready sh0_ready sh1_ready ahT_ready ends_ready arg_ready parts_ready "
            "q_ready head_step head_done y_ready hvar_ready yn_ready tail_step arg_step ln_step worst_ready good_step "
            "off_ready var0_ready rstd0_ready var1_ready rstd1_ready all_ready hbias_ready hb_ready xb_ready "
            "hve_ready hrstd_ready yg_ready out_ready bad_ready").split()}
        block = ctx.enter_context(nc.Block())

        def passes(eng, one_pass):
            one_pass(0, 0, True, False, False, True)
            one_pass(1, 1, True, True, False, True)
            last = B - 2 if B % 2 == 0 else B - 1
            if last > 2:
                with eng.Fori(2, last, 2) as g:
                    one_pass(g, 0, True, True, True, True)
                    one_pass(g + 1, 1, True, True, True, True)
            for g in range(max(last, 2), B + 2):
                one_pass(g, g % 2, g < B, g <= B, True, g + 1 < B)

        @block.sync
        def _(sp):
            def load_x(g, p):
                need(sp, S["xb_ready"], g - 1)
                need(sp, S["h1_ready"], g - 1)
                sp.dma_start(xs[p][:], x[g, :, :].rearrange("(r p) d -> p r d", p=P)).then_inc(S["x_in"], 16)

            def one_pass(g, p, do0, do1, do2, more):
                for r in range(R):
                    n = g * R + r
                    if do0:
                        need(sp, S["off_ready"], n - ADJ_RING + 1)
                        sp.dma_start(adj_t[r % ADJ_RING][:], adj[g, r * P:(r + 1) * P, :]).then_inc(S[f"adj{r % ADJ_RING}_in"], 16)
                    if r == 6 and more:
                        load_x(g + 1, 1 - p)
                    if r == 6 and do2:
                        need(sp, S["out_ready"], g - 1)
                        sp.dma_start(out[g - 2, :, :].rearrange("(r p) d -> p r d", p=P), y[:]).then_inc(S["out_stored"], 16)
            load_x(0, 0)
            passes(sp, one_pass)
            sp.wait_ge(S["out_stored"], 16 * B)

        @block.tensor
        def _(pe):
            def turn_h(g, p, c):
                if c == 0:
                    need(pe, S["h0_ready"], g + 1)
                    need(pe, S["t_ready"], g * R)
                else:
                    need(pe, S["hT_ready"], g * C + 1)
                for r in range(R):
                    last = pe.transpose(e_ps[:, r // 4, (r % 4) * P:(r % 4 + 1) * P], hs[p][:, r, c * P:(c + 1) * P], ident[:])
                last.then_inc(S["hT_psum"], 1)

            def scores(g, p, r):
                n = g * R + r
                if r == 0:
                    need(pe, S["hT_ready"], g * C + C)
                    need(pe, S["ahT_ready"], g * C + C)
                need(pe, S["t_ready"], n)
                for half_ in range(2):
                    cols = slice(half_ * 512, (half_ + 1) * 512)
                    for c in range(C):
                        pe.matmul(e_ps[:, half_, :], ahT[:, c, r * P:(r + 1) * P], hT[:, c, cols], start=(c == 0), stop=False)
                    if half_ == 0:
                        need(pe, S["off_ready"], n + 1)
                    last = pe.matmul(e_ps[:, half_, :], identb[:], off[r % ADJ_RING][:, cols], start=False, stop=True)
                last.then_inc(S["e_ready"], 1)
                need(pe, S["mt_ready"], n)
                if r == 5:
                    need(pe, S["ut_ready"], g)
                for j in range(R):
                    last = pe.transpose(m_ps[:, j * P:(j + 1) * P], off[r % ADJ_RING][:, j * P:(j + 1) * P], identb[:])
                last.then_inc(S["mt_psum"], 1)

            def turn_p(m, r, heads, spread_):
                need(pe, S["p_ready"], m + 1)
                need(pe, S["pt_ready"], m)
                need(pe, S["head_done"], heads)
                need(pe, S["ub_ready"], spread_)
                for j in range(R):
                    last = pe.transpose(t_ps[:, j // 4, (j % 4) * P:(j % 4 + 1) * P], ps[r % 2][:, j * P:(j + 1) * P], ident[:])
                last.then_inc(S["pt_psum"], 1)

            def sum0(m, p):
                need(pe, S["pt_ready"], m + 1)
                need(pe, S["x1_ready"], m)
                for j in range(R):
                    last = pe.matmul(o_ps[:, 0:D], pT[:, j, :], hs[p][:, j, :], start=(j == 0), stop=(j == R - 1))
                last.then_inc(S["o_ready"], 1)

            def turn_h1(g, c):
                if c == 0:
                    need(pe, S["h1_ready"], g + 1)
                    need(pe, S["nT_ready"], g * H)
                else:
                    need(pe, S["h1T_ready"], g * C + 1)
                for r in range(R):
                    last = pe.transpose(n_ps[:, r // 4, (r % 4) * P:(r % 4 + 1) * P], h1[:, r, c * P:(c + 1) * P], ident[:])
                last.then_inc(S["h1T_psum"], 1)

            def project(g):
                need(pe, S["h1T_ready"], g * C + C)
                for r in range(R):
                    if r >= 2:
                        need(pe, S["hw_ready"], g * R + r - 1)
                    for c in range(C):
                        last = pe.matmul(n_ps[:, r % 2, 0:WF], h1T[:, c, r * P:(r + 1) * P], wf[:, c, :],
                                         start=(c == 0), stop=(c == C - 1))
                    last.then_inc(S["pj_ready"], 1)

            def turn_u(g, n):
                need(pe, S["mt_ready"], n)
                need(pe, S["parts_ready"], g + 1)
                for r in range(R):
                    last = pe.transpose(m_ps[0:3 * H, r * P:(r + 1) * P], parts[:, r, :, :].rearrange("p k h -> p (k h)"), identb[:])
                last.then_inc(S["ut_psum"], 1)

            def spread_u(g, m, h):
                if h == 0:
                    need(pe, S["ut_ready"], g + 1)
                    need(pe, S["hw_ready"], g * R + R)
                    need(pe, S["pt_ready"], m)
                if h >= 2:
                    need(pe, S["ub_ready"], g * H + h - 1)
                for half_ in range(2):
                    last = pe.matmul((n_ps, t_ps)[h % 2][:, half_, :], pick[:, h, :], uT[:, half_ * 512:(half_ + 1) * 512],
                                     start=True, stop=True)
                last.then_inc(S["ub_psum"], 1)

            def unit(g, u):
                h, j = u // R, u % R
                need(pe, S["q_ready"], g * UNITS + u + 1)
                if u == 0:
                    need(pe, S["hb_ready"], g + 1)
                    need(pe, S["ub_ready"], g * H + H)
                if j == 0:
                    need(pe, S["nT_ready"], g * H + h)
                for half_ in range(2):
                    last = pe.matmul(n_ps[0:E + 1, half_, :], hb[:, j, h, :], qs[u % Q_RING][:, half_ * 512:(half_ + 1) * 512],
                                     start=(j == 0), stop=(j == R - 1))
                last.then_inc(S["unit_done"], 1)

            def turn_head(g, h, m):
                need(pe, S["nT_ready"], g * H + h + 1)
                need(pe, S["pt_ready"], m)
                for i in range(R):
                    last = pe.transpose(num()[:, i // 4, i % 4, :], nT[:, i * P:(i + 1) * P], ident[0:E + 1, 0:E + 1])
                last.then_inc(S["head_psum"], 1)

            def one_pass(g, p, do0, do1, do2, more):
                todo = list(range(UNITS)) if do1 else []

                def units(count_):
                    for _ in range(count_ if todo else 0):
                        unit(g - 1, todo.pop(0))

                for r in range(R):
                    n = g * R + r
                    m = n if do0 or (do1 and r == 0) else B * R
                    before = (do0 and r > 0) or (do1 and r == 0)
                    heads = (g - 1) * H - 1 if r == 0 else (g - 1) * H + max(r - 5, 0)
                    if before:
                        turn_p(n - 1, r - 1 if r else R - 1, heads, (g - 1) * H if r < 5 else g * H)
                    if do0:
                        scores(g, p, r)
                    if r == 0 and do2:
                        turn_head(g - 2, H - 1, m)
                    if do1:
                        if r == 2:
                            turn_h1(g - 1, 0)
                        if r == 3:
                            project(g - 1)
                        if r >= 5:
                            turn_head(g - 1, r - 5, m)
                    units(UNIT_PLAN[r][0])
                    if before:
                        sum0(n - 1, p if r else 1 - p)
                    if do1 and r == 2:
                        turn_h1(g - 1, 1)
                    if do1 and r == 4:
                        turn_u(g - 1, n + 1 if do0 else B * R)
                        for h in range(H):
                            spread_u(g - 1, m, h)
                    units(UNIT_PLAN[r][1])
                for c in range(C):
                    if more:
                        turn_h(g + 1, 1 - p, c)
                    units(END_PLAN[c])
                assert not todo
            turn_h(0, 0, 0)
            turn_h(0, 0, 1)
            passes(pe, one_pass)

        @block.scalar
        def _(act):
            def norm(g, xt, ht, shift_sig, done, rstd, shift, out_free, free_value):
                need(act, shift_sig, g + 1)
                need(act, out_free, free_value)
                for r in range(R):
                    last = act.activation(ht[:, r, :], xt[:, r, :], ACT.Relu, bias=shift[:, r:r + 1], scale=rstd[:, r:r + 1])
                last.then_inc(done, 1)

            def norm0(g, p):
                norm(g, xs[p], hs[p], S["sh0_ready"], S["h0_ready"], rstd0, shift0, S["o_ready"], g * R - R)

            def copy_hT(g, c):
                need(act, S["hT_psum"], g * C + c + 1)
                act.activation(hT[:, c, :], flat(e_ps[:]), ACT.Copy).then_inc(S["hT_ready"], 1)

            def positive(n):
                need(act, S["e_ready"], n + 1)
                need(act, S["t_ready"], n)
                act.activation(pos[:], flat(e_ps[:]), ACT.Relu, scale=4.0).then_inc(S["pos_ready"], 1)

            def copy_pT(m):
                need(act, S["pt_psum"], m + 1)
                need(act, S["o_ready"], m)
                act.activation(pT[:].rearrange("p j i -> p (j i)"), flat(t_ps[:]), ACT.Copy).then_inc(S["pt_ready"], 1)

            def copy_mT(g, p, r):
                need(act, S["mt_psum"], g * R + r + 1)
                if r == 0:
                    need(act, S["q_ready"], (g - 1) * UNITS)
                act.activation(mT[p][:, :, r * P:(r + 1) * P], m_ps[:].rearrange("p (j i) -> p j i", j=R), ACT.Identity,
                               bias=one[:], scale=1.0 / BIG).then_inc(S["mt_ready"], 1)

            def exponent(n, r):
                need(act, S["t_ready"], n + 1)
                need(act, S["x1_ready"], n - 1)
                act.activation(ps[r % 2][:], ps[r % 2][:], ACT.Exp, bias=nm[:, r:r + 1], scale=-1.0,
                               accum_out=rs[r % 2][:]).then_inc(S["p_ready"], 1)

            def copy_h1T(g, c):
                need(act, S["h1T_psum"], g * C + c + 1)
                act.activation(h1T[:, c, :], flat(n_ps[:]), ACT.Copy).then_inc(S["h1T_ready"], 1)

            def copy_hw(g, rows):
                if 0 in rows:
                    need(act, S["y_ready"], g)
                    need(act, S["hbias_ready"], g)
                for r in rows:
                    need(act, S["pj_ready"], g * R + r + 1)
                    act.activation(hw[:, r, :], n_ps[:, r % 2, 0:WF], ACT.Copy).then_inc(S["hw_ready"], 1)

            def factors(g):
                need(act, S["arg_ready"], g + 1)
                need(act, S["unit_done"], g * UNITS)
                act.activation(U[:], argc[:], ACT.Exp).then_inc(S["ex_ready"], 1)
                act.activation(hb[:, :, :, E], argb[:], ACT.Exp).then_inc(S["ex_ready"], 1)
                act.activation(V[:], argb[:], ACT.Exp, scale=-(1.0 - SLOPE1)).then_inc(S["ex_ready"], 1)

            def copy_u(g, h):
                if h == 0:
                    need(act, S["ut_psum"], g + 1)
                    need(act, S["q_ready"], g * UNITS)
                    act.activation(uT[:], m_ps[0:3 * H, :], ACT.Copy).then_inc(S["ut_ready"], 1)
                need(act, S["ub_psum"], g * H + h + 1)
                act.activation(ub[h][:], flat((n_ps, t_ps)[h % 2][:]), ACT.Copy).then_inc(S["ub_ready"], 1)

            def copy_head(g, h):
                need(act, S["unit_done"], g * UNITS + (h + 1) * R)
                need(act, S["head_psum"], g * H + h)
                act.activation(nT[:], flat(n_ps[0:E + 1]), ACT.Copy).then_inc(S["nT_ready"], 1)

            def one_pass(g, p, do0, do1, do2, more):
                for r in range(R):
                    n = g * R + r
                    if (do0 and r > 0) or (do1 and r == 0):
                        copy_pT(n - 1)
                    if do0:
                        positive(n)
                        copy_mT(g, p, r)
                    if do1 and r == 2:
                        copy_h1T(g - 1, 0)
                    if do1 and r == 3:
                        copy_hw(g - 1, range(2))
                    if do1 and r == 4:
                        factors(g - 1)
                    if do0:
                        exponent(n, r)
                    if do1 and r == 0:
                        norm(g - 1, xs[1 - p], h1, S["sh1_ready"], S["h1_ready"], rstd1, shift1, S["h1T_psum"], (g - 1) * C)
                    if do1 and r == 2:
                        copy_h1T(g - 1, 1)
                    if do1 and r == 3:
                        copy_hw(g - 1, range(2, R))
                    if do1 and r == 4:
                        for h in range(H):
                            copy_u(g - 1, h)
                    if r == 6 and more:
                        norm0(g + 1, 1 - p)
                    if do1 and 4 <= r < 7:
                        copy_head(g - 1, r - 4)
                if more:
                    copy_hT(g + 1, 0)
                    copy_hT(g + 1, 1)
                if do1:
                    copy_head(g - 1, H - 1)
            norm0(0, 0)
            copy_hT(0, 0)
            copy_hT(0, 1)
            passes(act, one_pass)

        @block.vector
        def _(dve):
            def stand(signal, value):
                if isinstance(value, int):
                    need(dve, signal, value)
                else:
                    dve.wait_ge(signal, value)
                    dve.memset(idle[:, bass.ts(next(turns) % 16, 1)], 0.0)

            def aggregate(mvx, stx, st_sig, step, value):
                stand(step, value)
                for r in range(R):
                    last = dve.bn_aggr(mvx[:, r, :], stx[:, r, :])
                last.then_inc(st_sig, 1)

            def shifted(g, mvx, rstd, shift, rstd_sig, sh_sig):
                need(dve, rstd_sig, g + 1)
                dve.scalar_tensor_tensor(shift[:], mvx[:, :, 0], -1.0, rstd[:], ALU.mult, ALU.mult).then_inc(sh_sig, 1)

            def stats0_(g, p):
                need(dve, S["x_in"], g * 16 + 16)
                need(dve, S["h0_ready"], g)
                for r in range(R):
                    last = dve.bn_stats(stats0[:, r, :], xs[p][:, r, :])
                last.then_inc(S["ln_step"], 1)
                aggregate(mv0, stats0, S["st0_ready"], S["ln_step"], g + 1)

            def scale_hT(g, c):
                need(dve, S["hT_ready"], g * C + c + 1)
                dve.tensor_scalar(ahT[:, c, :], hT[:, c, :], aT[:, c, 0:1], None, ALU.mult).then_inc(S["ahT_ready"], 1)

            def leaky(n, r):
                need(dve, S["pt_psum"], n - 1)
                stand(S["pos_ready"], n + 1)
                dve.tensor_tensor_reduce(ps[r % 2][:], flat(e_ps[:]), pos[:], -SLOPE0, 3.0e38, ALU.add, ALU.min,
                                         nm[:, r:r + 1]).then_inc(S["t_ready"], 1)

            def add0(m, p, r):
                need(dve, S["p_ready"], m + 1)
                dve.reciprocal(rinv[:], rs[r % 2][:]).then_inc(S["x1_step"], 1)
                need(dve, S["o_ready"], m + 1)
                need(dve, S["x1_step"], m + 1)
                dve.scalar_tensor_tensor(xs[p][:, r, :], o_ps[:, 0:D], rinv[:], xs[p][:, r, :], ALU.mult, ALU.add)\
                    .then_inc(S["x1_ready"], 1)
                need(dve, S["x1_ready"], m + 1)
                dve.bn_stats(stats1[:, r, :], xs[p][:, r, :]).then_inc(S["ln1_step"], 1)

            def arguments(g):
                need(dve, S["hw_ready"], g * R + R)
                d = hw[:, :, D + H:WF]
                dve.tensor_reduce(ends[:, 0:H], d.rearrange("p r h -> p h r"), AX_X, ALU.max)
                dve.tensor_reduce(ends[:, H:2 * H], d.rearrange("p r h -> p h r"), AX_X, ALU.min, negate=True).then_inc(S["ends_ready"], 1)
                need(dve, S["all_ready"], g + 1)
                top = all_ends[:, 0:H].unsqueeze(1).broadcast_to([P, R, H])
                dve.tensor_tensor(spread[:, bass.ds(g, 1), :].rearrange("p o h -> p (o h)"), all_ends[:, 0:H], all_ends[:, H:2 * H], ALU.add)\
                    .then_inc(S["good_step"], 1)
                dve.tensor_tensor(argd[:], d, top, ALU.subtract)
                dve.tensor_tensor(argu[:], hw[:, :, D:D + H], top, ALU.add).then_inc(S["arg_step"], 1)
                need(dve, S["arg_step"], g * 5 + 1)
                dve.tensor_scalar(argb[:], argd[:], -CAP, None, ALU.max)
                dve.tensor_scalar(argc[:], argu[:], 1.0 - SLOPE1, CAP, ALU.mult, ALU.min).then_inc(S["arg_ready"], 1)

            def split_u(g):
                need(dve, S["ex_ready"], g * 3 + 3)
                dve.tensor_copy(parts[:, :, 0, :], U[:]).then_inc(S["arg_step"], 1)
                need(dve, S["arg_step"], g * 5 + 2)
                dve.tensor_tensor(rest[:, 0], U[:], parts[:, :, 0, :], ALU.subtract).then_inc(S["arg_step"], 1)
                need(dve, S["arg_step"], g * 5 + 3)
                dve.tensor_copy(parts[:, :, 1, :], rest[:, 0]).then_inc(S["arg_step"], 1)
                need(dve, S["arg_step"], g * 5 + 4)
                dve.tensor_tensor(rest[:, 1], rest[:, 0], parts[:, :, 1, :], ALU.subtract).then_inc(S["arg_step"], 1)
                need(dve, S["arg_step"], g * 5 + 5)
                dve.tensor_copy(parts[:, :, 2, :], rest[:, 1]).then_inc(S["parts_ready"], 1)

            def weigh(g, p, u):
                h, j = u // R, u % R
                if j == 0:
                    need(dve, S["ub_ready"], g * H + h + 1)
                if u == 0:
                    need(dve, S["mt_ready"], g * R + R)
                need(dve, S["unit_done"], g * UNITS + u - Q_RING + 1)
                dve.scalar_tensor_tensor(qs[u % Q_RING][:], ub[h][:], V[:, j, h:h + 1], mT[p][:, j, :], ALU.max, ALU.mult)\
                    .then_inc(S["q_ready"], 1)

            def head(g, h):
                need(dve, S["head_psum"], g * H + h + 1)
                dve.tensor_scalar(nsum[:].rearrange("p (a r) -> p a r", a=2), num()[:, :, :, E], TINY, None, ALU.max)\
                    .then_inc(S["head_step"], 1)
                need(dve, S["head_step"], (g * H + h) * 2 + 1)
                dve.reciprocal(ninv[:], nsum[:]).then_inc(S["head_step"], 1)
                if h == 0:
                    need(dve, S["out_stored"], g * 16)
                need(dve, S["head_step"], (g * H + h) * 2 + 2)
                dve.tensor_tensor(y[:, :, h * E:(h + 1) * E].rearrange("p (a r) e -> p a r e", a=2), num()[:, :, :, 0:E],
                                  ninv[:].rearrange("p (a r) -> p a r", a=2).unsqueeze(3).broadcast_to([P, 2, 4, E]), ALU.mult)\
                    .then_inc(S["head_done"], 1)

            def add1(g):
                need(dve, S["head_done"], g * H + H)
                dve.scalar_tensor_tensor(y[:], y[:], 0.0, hw[:, :, 0:D], ALU.max, ALU.add).then_inc(S["y_ready"], 1)

            def tail_stats(g):
                need(dve, S["y_ready"], g + 1)
                for i in range(R * H):
                    last = dve.bn_stats(hst[:, i, :], y[:, i // H, (i % H) * E:(i % H + 1) * E])
                last.then_inc(S["tail_step"], 1)
                need(dve, S["tail_step"], g * 4 + 1)
                dve.tensor_tensor(hsum[:], hst[:, :, 1], hst[:, :, 4], ALU.add)
                dve.tensor_tensor(hdif[:], hst[:, :, 1], hst[:, :, 4], ALU.subtract)
                dve.tensor_tensor(hm2[:], hst[:, :, 2], hst[:, :, 5], ALU.add).then_inc(S["tail_step"], 1)
                need(dve, S["tail_step"], g * 4 + 2)
                dve.scalar_tensor_tensor(hsq[:], hdif[:], 0.25, hdif[:], ALU.mult, ALU.mult).then_inc(S["tail_step"], 1)
                need(dve, S["tail_step"], g * 4 + 3)
                dve.scalar_tensor_tensor(hvar[:], hm2[:], 1.0 / E, hsq[:], ALU.mult, ALU.add).then_inc(S["hvar_ready"], 1)

            wide = lambda a: a[:].unsqueeze(2).broadcast_to([P, R * H, E])
            ye = y[:].rearrange("p r (h e) -> p (r h) e", h=H)

            def tail_centre(g):
                dve.scalar_tensor_tensor(ye, wide(hsum), -0.5, ye, ALU.mult, ALU.add).then_inc(S["tail_step"], 1)

            def tail_norm(g):
                need(dve, S["hrstd_ready"], g + 1)
                need(dve, S["tail_step"], g * 4 + 4)
                dve.tensor_tensor(ye, ye, wide(hrstd), ALU.mult).then_inc(S["yn_ready"], 1)

            def one_pass(g, p, do0, do1, do2, more):
                todo = list(range(UNITS)) if do1 else []

                def units(count_):
                    for _ in range(count_ if todo else 0):
                        weigh(g - 1, 1 - p, todo.pop(0))

                for r in range(R):
                    n = g * R + r
                    units(UNIT_PLAN[r][0])
                    if do0:
                        leaky(n, r)
                    if do1 and r == 4:
                        split_u(g - 1)
                    if do1 and r >= 5:
                        head(g - 1, r - 5)
                    if do2 and r == 0:
                        head(g - 2, H - 1)
                    ahead = min(UNIT_PLAN[r][1], Q_RING)
                    units(ahead)
                    if (do0 and r > 0) or (do1 and r == 0):
                        add0(n - 1, p if r else 1 - p, r - 1 if r else R - 1)
                    if do1 and r == 0:
                        need(dve, S["h1_ready"], g - 1)
                        aggregate(mv1, stats1, S["st1_ready"], S["ln1_step"], g * R)
                    if do2 and r == 0:
                        add1(g - 2)
                    if do1 and r == 0:
                        shifted(g - 1, mv1, rstd1, shift1, S["rstd1_ready"], S["sh1_ready"])
                    if do2 and r == 0:
                        tail_stats(g - 2)
                    if do2 and r == 1:
                        tail_centre(g - 2)
                    if do2 and r == 2:
                        tail_norm(g - 2)
                    if do1 and r == 3:
                        arguments(g - 1)
                    if r == 5 and more:
                        stats0_(g + 1, 1 - p)
                    units(UNIT_PLAN[r][1] - ahead)
                    if r == 5 and more:
                        shifted(g + 1, mv0, rstd0, shift0, S["rstd0_ready"], S["sh0_ready"])
                if do0:
                    stand(S["t_ready"], g * R + R)
                    dve.tensor_reduce(worst[:, bass.ds(g, 1)], nm[:], AX_X, ALU.max, apply_absolute_value=True)\
                        .then_inc(S["worst_ready"], 1)
                for c in range(C):
                    if more:
                        scale_hT(g + 1, c)
                    units(END_PLAN[c])
            stats0_(0, 0)
            shifted(0, mv0, rstd0, shift0, S["rstd0_ready"], S["sh0_ready"])
            scale_hT(0, 0)
            scale_hT(0, 1)
            passes(dve, one_pass)
            dve.wait_ge(S["worst_ready"], B)
            dve.wait_ge(S["good_step"], B)
            dve.tensor_scalar(good[:, 0:B], worst[:], LIMIT, None, ALU.is_lt)
            dve.tensor_scalar(good[:, B:], spread[:].rearrange("p g h -> p (g h)"), SPREAD, None, ALU.is_le).then_inc(S["good_step"], 1)
            dve.wait_ge(S["good_step"], B + 1)
            dve.tensor_reduce(bad[:, 0:1], good[:], AX_X, ALU.min).then_inc(S["good_step"], 1)
            dve.wait_ge(S["good_step"], B + 2)
            dve.tensor_scalar(bad[:, 0:1], bad[:, 0:1], -1.0, 1.0, ALU.mult, ALU.add).then_inc(S["good_step"], 1)
            dve.wait_ge(S["bad_ready"], 1)
            dve.tensor_copy(flag, bad[0:1, 1:2])

        @block.gpsimd
        def _(pool):
            def stand(signal, value):
                if isinstance(value, int):
                    need(pool, signal, value)
                else:
                    pool.wait_ge(signal, value)
                    pool.tensor_tensor(idle_p[:, bass.ts(next(turns) % 16, 1)], one[:], one[:], ALU.add)

            def inverse_root(g, var, eps_col, signal, ve, ve_ready, out_, ready, n):
                need(pool, signal, g + 1)
                pool.tensor_tensor(ve[:], var, eps[:, eps_col:eps_col + 1].broadcast_to([P, n]), ALU.add).then_inc(ve_ready, 1)
                need(pool, ve_ready, g + 1)
                pool.tensor_tensor(out_[:], ve[:], half[:, 0:n], ALU.pow).then_inc(ready, 1)

            def root0(g):
                inverse_root(g, mv0[:, :, 1], 0, S["st0_ready"], var0, S["var0_ready"], rstd0, S["rstd0_ready"], R)

            def missing(n, g, r):
                need(pool, S["mt_psum"], n - ADJ_RING + 1)
                stand(S[f"adj{r % ADJ_RING}_in"], g * (16 * R // ADJ_RING) + (r // ADJ_RING + 1) * 16)
                pool.tensor_scalar(off[r % ADJ_RING][:], adj_t[r % ADJ_RING][:].bitcast(U32), BIG, -BIG, ALU.mult, ALU.add)\
                    .then_inc(S["off_ready"], 1)

            by_head = lambda a: a.rearrange("p r (h e) -> p r h e", h=H)
            over_rows = lambda i: bgb[:, i, :].unsqueeze(1).broadcast_to([P, R, D])

            def ends_all(g):
                stand(S["ends_ready"], g + 1)
                pool.partition_all_reduce(all_ends[:], ends[:], P, bass.bass_isa.ReduceOp.max).then_inc(S["all_ready"], 1)

            def add_bias(g):
                need(pool, S["unit_done"], g * UNITS)
                need(pool, S["hw_ready"], g * R + R)
                pool.tensor_tensor(hb[:, :, :, 0:E], by_head(hw[:, :, 0:D]), by_head(over_rows(0)), ALU.add).then_inc(S["hbias_ready"], 1)

            def weigh_h(g):
                need(pool, S["ex_ready"], g * 3 + 2)
                need(pool, S["hbias_ready"], g + 1)
                pool.tensor_tensor(hb[:, :, :, 0:E], hb[:, :, :, 0:E], hb[:, :, :, E:E + 1].broadcast_to([P, R, H, E]), ALU.mult)\
                    .then_inc(S["hb_ready"], 1)

            def residual(g, p):
                need(pool, S["out_ready"], g)
                need(pool, S["x1_ready"], g * R + R)
                pool.tensor_tensor(xb[:], xs[p][:], over_rows(2), ALU.add).then_inc(S["xb_ready"], 1)

            def tail_gamma(g):
                need(pool, S["yn_ready"], g + 1)
                pool.tensor_tensor(y[:], y[:], over_rows(1), ALU.mult).then_inc(S["yg_ready"], 1)

            def tail_add(g):
                need(pool, S["yg_ready"], g + 1)
                need(pool, S["xb_ready"], g + 1)
                pool.tensor_tensor(y[:], y[:], xb[:], ALU.add).then_inc(S["out_ready"], 1)

            def one_pass(g, p, do0, do1, do2, more):
                for r in range(R):
                    n = g * R + r
                    if do0 and (r + 1 < R or more):
                        missing(n + 1, g if r + 1 < R else g + 1, (r + 1) % R)
                    if do1 and r == 0:
                        inverse_root(g - 1, mv1[:, :, 1], 0, S["st1_ready"], var1, S["var1_ready"], rstd1, S["rstd1_ready"], R)
                    if do2 and r == 0:
                        inverse_root(g - 2, hvar[:], 1, S["hvar_ready"], hve, S["hve_ready"], hrstd, S["hrstd_ready"], R * H)
                    if do2 and r == 2:
                        tail_gamma(g - 2)
                    if do2 and r == 3:
                        tail_add(g - 2)
                    if do1 and r == 3:
                        ends_all(g - 1)
                        add_bias(g - 1)
                    if do1 and r == 4:
                        weigh_h(g - 1)
                    if do1 and r == 5:
                        residual(g - 1, 1 - p)
                    if more and r == 5:
                        root0(g + 1)
            root0(0)
            missing(0, 0, 0)
            passes(pool, one_pass)
            pool.wait_ge(S["good_step"], B + 3)
            pool.partition_all_reduce(bad[:, 1:2], bad[:, 0:1], P, bass.bass_isa.ReduceOp.max).then_inc(S["bad_ready"], 1)


def program(nc, ins, out):
    with ExitStack() as ctx:
        k = constants(nc, ctx, ins)
        flag = ctx.enter_context(nc.sbuf_tensor("flag", [1, 1], I32))[:]
        plain_path(nc, k, ins, out, flag)
        general_path(nc, k, ins, out, flag)


_INS = ["x", "adj", "L0_gnn_a_0", "L0_gnn_a_1", "L0_gnn_a_2", "L0_gnn_a_3", "L1_gnn_W", "L1_gnn_a_src",
        "L1_gnn_a_dst", "L1_gnn_bias", "L1_gnn_ln_gamma", "L1_gnn_ln_beta"]


def kernel(**inputs):
    import numpy as _np
    import concourse.bacc as _bacc
    from concourse import mybir as _mybir
    from concourse.bass_utils import run_bass_kernel_spmd as _run

    nc = _bacc.Bacc("TRN2", target_bir_lowering=False, num_devices=1)
    arrays, aps = {}, {}
    for name in _INS:
        a = _np.ascontiguousarray(inputs[name])
        arrays[f"in_{name}"] = a
        aps[name] = nc.dram_tensor(f"in_{name}", a.shape, _mybir.dt.from_np(a.dtype), kind="ExternalInput").ap()
    out = nc.dram_tensor("out_0", (B, N, D), F32, kind="ExternalOutput").ap()
    program(nc, aps, out)
    r = _run(nc, [arrays], core_ids=[0])
    return r.results[0]["out_0"]
```

```python
from contextlib import ExitStack
from itertools import count

import concourse.bass as bass
from concourse import mybir

ALU = mybir.AluOpType
ACT = mybir.ActivationFunctionType
F32 = mybir.dt.float32
F32R = mybir.dt.float32r
BF16 = mybir.dt.bfloat16
I32 = mybir.dt.int32
U8 = mybir.dt.uint8
U32 = mybir.dt.uint32
AX_X = mybir.AxisListType.X

P = 128
B, N, D = 16, 1024, 256
R = N // P
C = D // P
K0 = 4
H, E, T1 = 4, 64, 5
HT = H * T1
WN = D + 2 * HT
WF = D + 2 * H
LN_EPS = 1e-5
HEAD_EPS = 1e-6
SLOPE0, SLOPE1 = 0.2, 0.01
NEG0, NEG1 = -9000000000000000.0, -1000000000.0
BIG = 2.0 ** 90
SPREAD = 40.0
CAP = 44.0
UNITS = R * H
Q_RING = 4
ADJ_RING = 2
TINY = 2.0 ** -100
LIMIT = 2.0 ** 50
DEPTH = 2.0 ** -22
HI_LO = ("hi", "lo")
PRODUCTS = ((0, 0), (1, 0), (0, 1))
UNIT_PLAN = [(0, 0)] * 4 + [(0, 8), (4, 4), (4, 4), (4, 0)]
END_PLAN = (2, 2)


class Steps:

    def __init__(self, eng, sem, start=0):
        self.eng, self.sem, self.start, self.n = eng, sem, start, 0

    def did(self, ins):
        ins.then_inc(self.sem, 1)
        self.n += 1

    def settle(self):
        self.eng.wait_ge(self.sem, self.start + self.n)


def constants(nc, ctx, ins):
    sb = lambda name, shape, dt: ctx.enter_context(nc.sbuf_tensor(name, shape, dt))
    sem = lambda name: ctx.enter_context(nc.semaphore(name))
    k = {
        "ident": sb("ident", [P, P], F32),
        "aT": sb("aT", [P, C, K0], F32),
        "wa": sb("wa", [P, C, WN], F32),
        "bgb": sb("bgb", [P, 3, D], F32),
        "eps": sb("eps", [P, 2], F32),
        "identb": sb("identb", [P, P], BF16),
        "one": sb("one", [P, 1], F32),
        "half": sb("half", [P, R * H], F32),
        "pick": sb("pick", [3 * H, H, P], BF16),
        "wf": sb("wf", [P, C, WF], F32),
    }
    identb, one, half, pick, wf = (k[n] for n in ("identb", "one", "half", "pick", "wf"))
    ident, aT, wa, bgb, eps = (k[n] for n in ("ident", "aT", "wa", "bgb", "eps"))
    with ExitStack() as own:
        tb = lambda name, shape, dt: own.enter_context(nc.sbuf_tensor(name, shape, dt))
        pb = lambda name, shape: own.enter_context(nc.psum_tensor(name, shape, F32))
        sm = lambda name: own.enter_context(nc.semaphore(name))
        attn_rows = tb("attn_rows", [2 * HT, E], F32)
        attn_cols = tb("attn_cols", [E, 2 * HT], F32)
        wT = tb("wT", [E, H, D], F32)
        rows = tb("rows", [1, 3, D], F32)
        ones = tb("ones", [1, P], F32)
        ps_wT = pb("ps_wT", [P, 2, 512])
        ps_wa = pb("ps_wa", [P, C, 2 * HT])
        ps_rows = pb("ps_rows", [P, 2, 512])
        ps_at = pb("ps_at", [P, 512])
        w_in, rows_in, attn_in = sm("w_in"), sm("rows_in"), sm("attn_in")
        filled, ident_ready, turned, turned_out, folded, spread = (
            sm(n) for n in ("filled", "ident_ready", "turned", "turned_out", "folded", "spread"))
        block = own.enter_context(nc.Block())

        @block.sync
        def _(sp):
            for h in range(H):
                sp.dma_start(wa[:, :, h * E:(h + 1) * E],
                             ins["L1_gnn_W"][h].rearrange("(c p) e -> p c e", p=P)).then_inc(w_in, 16)
            for k_, name in enumerate(["L0_gnn_a_0", "L0_gnn_a_1", "L0_gnn_a_2", "L0_gnn_a_3"]):
                sp.dma_start(aT[:, :, k_:k_ + 1],
                             ins[name].rearrange("(c p) o -> p c o", p=P),
                             allow_slow_non_contiguous=True).then_inc(w_in, 16)
            sp.wait_ge(w_in, 16 * (H + K0))

        @block.scalar
        def _(act):
            for i, name in enumerate(["L1_gnn_a_src", "L1_gnn_a_dst"]):
                act.dma_start(attn_rows[i * HT:(i + 1) * HT, :],
                              ins[name].rearrange("h t e -> (h t) e")).then_inc(attn_in, 16)
            for i, name in enumerate(["L1_gnn_bias", "L1_gnn_ln_gamma", "L1_gnn_ln_beta"]):
                act.dma_start(rows[:, i, :], ins[name].rearrange("(o h) e -> o (h e)", o=1)).then_inc(rows_in, 16)
            act.wait_ge(rows_in, 48)

        @block.gpsimd
        def _(pool):
            pool.memset(ident[:], 0.0).then_inc(filled, 1)
            pool.memset(ones[:], 1.0).then_inc(filled, 1)
            pool.memset(eps[:, 0:1], LN_EPS).then_inc(filled, 1)
            pool.memset(eps[:, 1:2], HEAD_EPS).then_inc(filled, 1)
            pool.memset(one[:], 1.0).then_inc(filled, 1)
            pool.memset(half[:], -0.5).then_inc(filled, 1)
            pool.memset(pick[:], 0.0).then_inc(filled, 1)
            pool.wait_ge(filled, 7)
            pool.affine_select(out=ident[:], in_=ident[:], compare_op=ALU.not_equal, fill=1.0, base=0,
                               pattern=[[-1, P]], channel_multiplier=1).then_inc(ident_ready, 1)
            pool.wait_ge(ident_ready, 1)
            pool.tensor_copy(identb[:], ident[:]).then_inc(ident_ready, 1)
            for part in range(3):
                pool.affine_select(out=pick[:], in_=pick[:], compare_op=ALU.not_equal, fill=1.0, base=-part * H,
                                   pattern=[[-1, H], [0, P]], channel_multiplier=1).then_inc(ident_ready, 1)
                pool.wait_ge(ident_ready, 3 + part)

        @block.tensor
        def _(pe):
            pe.wait_ge(ident_ready, 1)
            pe.wait_ge(w_in, 16 * (H + K0))
            pe.wait_ge(attn_in, 32)
            for h in range(H):
                for c in range(C):
                    last = pe.transpose(ps_wT[0:E, h // 2, (h % 2) * D + c * P:(h % 2) * D + (c + 1) * P],
                                        wa[:, c, h * E:(h + 1) * E], ident[:])
            last = pe.transpose(ps_at[0:E, 0:2 * HT], attn_rows[:], ident[0:2 * HT, 0:2 * HT])
            last.then_inc(turned, 1)
            pe.wait_ge(rows_in, 48)
            pe.wait_ge(filled, 7)
            flat = rows[:, :, :].rearrange("p a d -> p (a d)")
            pe.matmul(ps_rows[:, 0, :], ones[:], flat[:, 0:512], start=True, stop=True)
            pe.matmul(ps_rows[:, 1, 0:D], ones[:], flat[:, 512:768], start=True, stop=True).then_inc(spread, 1)
            pe.wait_ge(turned_out, 2)
            for c in range(C):
                for h in range(H):
                    for s in range(2):
                        col = s * HT + h * T1
                        last = pe.matmul(ps_wa[:, c, col:col + T1], wT[:, h, c * P:(c + 1) * P],
                                         attn_cols[:, col:col + T1], start=True, stop=True)
            last.then_inc(folded, 1)

        @block.vector
        def _(dve):
            dve.wait_ge(turned, 1)
            dve.tensor_copy(wT[:].rearrange("p (a b) d -> p a (b d)", a=2), ps_wT[0:E, :, :]).then_inc(turned_out, 1)
            dve.tensor_copy(attn_cols[:], ps_at[0:E, 0:2 * HT]).then_inc(turned_out, 1)
            dve.wait_ge(spread, 1)
            flat = bgb[:].rearrange("p a d -> p (a d)")
            dve.tensor_copy(flat[:, 0:512], ps_rows[:, 0, :])
            dve.tensor_copy(flat[:, 512:768], ps_rows[:, 1, 0:D])
            dve.wait_ge(folded, 1)
            dve.tensor_copy(wa[:, :, D:WN], ps_wa[:]).then_inc(folded, 1)
            dve.wait_ge(folded, 2)
            dve.tensor_copy(wf[:, :, 0:D], wa[:, :, 0:D])
            for s in range(2):
                dve.tensor_copy(wf[:, :, D + s * H:D + (s + 1) * H],
                                wa[:, :, D + s * HT:D + (s + 1) * HT].rearrange("p c (h t) -> p c h t", h=H)[:, :, :, 0])
    return k


def general_path(nc, k, ins, out, flag):
    x, adj = ins["x"], ins["adj"]
    ident, aT, wa, bgb, eps = (k[n] for n in ("ident", "aT", "wa", "bgb", "eps"))
    with ExitStack() as ctx:
        sb = lambda name, shape, dt: ctx.enter_context(nc.sbuf_tensor("g_" + name, shape, dt))
        pb = lambda name, shape: ctx.enter_context(nc.psum_tensor("g_" + name, shape, F32))
        sem = lambda name: ctx.enter_context(nc.semaphore("g_" + name))
        xs = sb("xs", [P, R, D], F32)
        hs = sb("hs", [P, R, D], F32)
        hT = sb("hT", [P, C, N], F32)
        stats = sb("stats", [P, R, 6], F32)
        mv = sb("mv", [P, R, 2], F32)
        sd = sb("sd", [P, R], F32)
        rstd = sb("rstd", [P, R], F32)
        shift = sb("shift", [P, R], F32)
        adj_t = sb("adj_t", [P, N], I32)
        masks = sb("masks", [P, T1 + 1, N], U8)
        lhs = sb("lhs", [P, K0, C, P], F32)
        S = sb("S", [P, N], F32)
        tmp = sb("tmp", [P, N], F32)
        probs = sb("probs", [P, N], F32)
        pT = sb("pT", [P, R, P], F32)
        neg = sb("neg", [P, N], F32)
        nm = sb("nm", [P, 1], F32)
        rs = sb("rs", [P, 1], F32)
        rinv = sb("rinv", [P, 1], F32)
        hw = sb("hw", [P, R, WN], F32)
        hwt = sb("hwt", [P, WN], F32)
        eT = sb("eT", [2 * HT, N], F32)
        dst = sb("dst", [P, HT, N], F32)
        ot = sb("ot", [P, D], F32)
        hst = sb("hst", [P, H, 6], F32)
        hmv = sb("hmv", [P, H, 2], F32)
        hsd = sb("hsd", [P, H], F32)
        hrs = sb("hrs", [P, H], F32)
        ps_e = pb("ps_e", [P, 4, 512])
        ps_t = pb("ps_t", [P, 2, 512])
        ps_o = pb("ps_o", [P, 512])

        x_in, adj_in, masked = sem("x_in"), sem("adj_in"), sem("masked")
        stats_ready, sd_ready, norm_ready, h_ready = sem("stats_ready"), sem("sd_ready"), sem("norm_ready"), sem("h_ready")
        hT_psum, hT_ready = sem("hT_psum"), sem("hT_ready")
        ln_step, t0_step, t1_step = sem("ln_step"), sem("t0_step"), sem("t1_step")
        lhs_ready, e_ready, e_copied, e_used = sem("lhs_ready"), sem("e_ready"), sem("e_copied"), sem("e_used")
        m_ready, p_ready, pt_psum, pT_ready = sem("m_ready"), sem("p_ready"), sem("pt_psum"), sem("pT_ready")
        o_ready, o_used = sem("o_ready"), sem("o_used")
        proj_ready, proj_used, row_ready, row_used = sem("proj_ready"), sem("proj_used"), sem("row_ready"), sem("row_used")
        src_ready, z_ready, z_used = sem("src_ready"), sem("z_ready"), sem("z_used")
        m1_ready, p1_ready, pt1_psum, pt1_ready, o1_ready, o1_used = (
            sem(n) for n in ("m1_ready", "p1_ready", "pt1_psum", "pt1_ready", "o1_ready", "o1_used"))
        hst_ready, hsd_ready, out_ready, out_stored = sem("hst_ready"), sem("hsd_ready"), sem("out_ready"), sem("out_stored")
        sel = sb("sel", [2 * HT, HT, P], F32)
        idle = sb("idle", [P, 1], F32)
        sel_zero, sel_ready = sem("sel_zero"), sem("sel_ready")
        neg_ready = sem("neg_ready")
        block = ctx.enter_context(nc.Block())

        def stand(signal, value):
            nc.vector.wait_ge(signal, value)
            nc.vector.memset(idle[:], 0.0)

        def guarded(eng, body):
            if flag is None:
                body()
            else:
                need = eng.value_load(flag, min_val=0, max_val=1)
                with eng.If(need > 0):
                    body()

        @block.sync
        def _(sp):
            def body():
                with sp.Fori(0, B) as b:
                    sp.wait_ge(out_stored, b * (16 * R) + 1)
                    sp.dma_start(xs[:], x[b, :, :].rearrange("(r p) d -> p r d", p=P)).then_inc(x_in, 16)
                    for layer in range(2):
                        with sp.Fori(0, R) as t:
                            sp.wait_ge(masked, b * (2 * R) + layer * R + t + 1)
                            sp.dma_start(adj_t[:], adj[b, bass.ts(t, P), :]).then_inc(adj_in, 16)
                            if layer:
                                sp.wait_ge(out_ready, b * R + t + 1)
                                sp.dma_start(out[b, bass.ts(t, P), :], ot[:]).then_inc(out_stored, 16)
                sp.wait_ge(out_stored, 16 * R * B + 1)
            guarded(sp, body)

        @block.gpsimd
        def _(pool):
            def body():
                pool.memset(sel[:], 0.0).then_inc(sel_zero, 1)
                pool.wait_ge(sel_zero, 1)
                pool.affine_select(out=sel[:], in_=sel[:], compare_op=ALU.not_equal, fill=1.0, base=-HT,
                                   pattern=[[-1, HT], [0, P]], channel_multiplier=1).then_inc(sel_ready, 1)
            guarded(pool, body)

        @block.tensor
        def _(pe):
            def transpose_h(n):
                pe.wait_ge(h_ready, n)
                for r in range(R):
                    for c in range(C):
                        last = pe.transpose(ps_e[:, 2 * c + r // 4, (r % 4) * P:(r % 4 + 1) * P],
                                            hs[:, r, c * P:(c + 1) * P], ident[:])
                last.then_inc(hT_psum, 1)

            def transpose_p():
                for j in range(R):
                    last = pe.transpose(ps_t[:, j // 4, (j % 4) * P:(j % 4 + 1) * P],
                                        probs[:, j * P:(j + 1) * P], ident[:])
                return last

            def body():
                pe.wait_ge(sel_ready, 1)
                with pe.Fori(0, B) as b:
                    transpose_h(b * 2 + 1)
                    with pe.Fori(0, R) as t:
                        n = b * R + t
                        pe.wait_ge(hT_ready, b * 2 + 1)
                        pe.wait_ge(lhs_ready, n + 1)
                        for q in range(K0):
                            pe.wait_ge(e_used, n * K0 + max(q - 1, 0) + 1)
                            for half in range(2):
                                for c in range(C):
                                    last = pe.matmul(ps_e[:, 2 * (q % 2) + half, :], lhs[:, q, c, :],
                                                     hT[:, c, half * 512:(half + 1) * 512],
                                                     start=(c == 0), stop=(c == C - 1))
                            last.then_inc(e_ready, 1)
                        pe.wait_ge(p_ready, n + 1)
                        transpose_p().then_inc(pt_psum, 1)
                        pe.wait_ge(pT_ready, n + 1)
                        for j in range(R):
                            last = pe.matmul(ps_o[:, 0:D], pT[:, j, :], hs[:, j, :],
                                             start=(j == 0), stop=(j == R - 1))
                        last.then_inc(o_ready, 1)
                    transpose_h(b * 2 + 2)
                    pe.wait_ge(hT_ready, b * 2 + 2)
                    for r in range(R):
                        if r >= 4:
                            pe.wait_ge(proj_used, b * R + r - 3)
                        for c in range(C):
                            last = pe.matmul(ps_e[:, r % 4, 0:WN], hT[:, c, r * P:(r + 1) * P], wa[:, c, :],
                                             start=(c == 0), stop=(c == C - 1))
                        last.then_inc(proj_ready, 1)
                    for half in range(2):
                        for c in range(C):
                            last = pe.matmul(ps_t[0:2 * HT, half, :], wa[:, c, D:WN],
                                             hT[:, c, half * 512:(half + 1) * 512],
                                             start=(c == 0), stop=(c == C - 1))
                    last.then_inc(row_ready, 1)
                    pe.wait_ge(row_used, b * (HT + 1) + 1)
                    pe.wait_ge(proj_used, b * R + R)
                    for r in range(HT):
                        if r >= 2:
                            pe.wait_ge(row_used, b * (HT + 1) + r)
                        for half in range(2):
                            last = pe.matmul(ps_e[:, 2 * (r % 2) + half, :], sel[:, r, :],
                                             eT[:, half * 512:(half + 1) * 512], start=True, stop=True)
                        last.then_inc(row_ready, 1)
                    with pe.Fori(0, R) as t:
                        for h in range(H):
                            n = b * (R * H) + t * H + h
                            pe.wait_ge(p1_ready, n + 1)
                            transpose_p().then_inc(pt1_psum, 1)
                            pe.wait_ge(pt1_ready, n + 1)
                            pe.wait_ge(o1_used, b * (R * H) + t * H + 1)
                            for j in range(R):
                                last = pe.matmul(ps_o[:, h * E:(h + 1) * E], pT[:, j, :],
                                                 hw[:, j, h * E:(h + 1) * E], start=(j == 0), stop=(j == R - 1))
                            last.then_inc(o1_ready, 1)
            guarded(pe, body)

        @block.scalar
        def _(act):
            def norm(n):
                act.wait_ge(stats_ready, n)
                act.activation(sd[:], mv[:, :, 1], ACT.Sqrt, bias=eps[:, 0:1]).then_inc(sd_ready, 1)
                act.wait_ge(norm_ready, n)
                for r in range(R):
                    last = act.activation(hs[:, r, :], xs[:, r, :], ACT.Relu,
                                          bias=shift[:, r:r + 1], scale=rstd[:, r:r + 1])
                last.then_inc(h_ready, 1)

            def body():
                with act.Fori(0, B) as b:
                    norm(b * 2 + 1)
                    with act.Fori(0, R) as t:
                        n = b * R + t
                        for q in range(K0):
                            act.wait_ge(e_ready, n * K0 + q + 1)
                            act.wait_ge(e_used, n * K0 + q + 1)
                            act.activation(tmp[:], ps_e[:, 2 * (q % 2):2 * (q % 2) + 2, :].rearrange("p a n -> p (a n)"),
                                           ACT.Copy).then_inc(e_copied, 1)
                        act.wait_ge(m_ready, n + 1)
                        act.activation(probs[:], S[:], ACT.Exp, bias=nm[:], accum_out=rs[:]).then_inc(p_ready, 1)
                        act.wait_ge(pt_psum, n + 1)
                        act.activation(pT[:].rearrange("p j i -> p (j i)"), ps_t[:].rearrange("p a n -> p (a n)"),
                                       ACT.Copy).then_inc(pT_ready, 1)
                    norm(b * 2 + 2)
                    act.wait_ge(row_ready, b * (HT + 1) + 1)
                    act.activation(eT[:], ps_t[0:2 * HT].rearrange("p a n -> p (a n)"), ACT.Copy).then_inc(row_used, 1)
                    for r in range(HT):
                        act.wait_ge(row_ready, b * (HT + 1) + r + 2)
                        act.activation(dst[:, r, :], ps_e[:, 2 * (r % 2):2 * (r % 2) + 2, :].rearrange("p a n -> p (a n)"),
                                       ACT.Copy).then_inc(row_used, 1)
                    act.wait_ge(row_used, b * (HT + 1) + HT + 1)
                    with act.Fori(0, R) as t:
                        act.wait_ge(src_ready, b * R + t + 1)
                        for h in range(H):
                            n = b * (R * H) + t * H + h
                            for q in range(T1):
                                act.wait_ge(z_used, n * T1 + q + 1)
                                col = D + h * T1 + q
                                act.activation(tmp[:], dst[:, h * T1 + q, :], ACT.Identity,
                                               bias=hwt[:, col:col + 1]).then_inc(z_ready, 1)
                            act.wait_ge(m1_ready, n + 1)
                            act.activation(probs[:], S[:], ACT.Exp, bias=nm[:], accum_out=rs[:]).then_inc(p1_ready, 1)
                            act.wait_ge(pt1_psum, n + 1)
                            act.activation(pT[:].rearrange("p j i -> p (j i)"), ps_t[:].rearrange("p a n -> p (a n)"),
                                           ACT.Copy).then_inc(pt1_ready, 1)
                        act.wait_ge(hst_ready, b * R + t + 1)
                        act.activation(hsd[:], hmv[:, :, 1], ACT.Sqrt, bias=eps[:, 1:2]).then_inc(hsd_ready, 1)
            guarded(act, body)

        LN_STEPS, T0_STEPS, T1_STEPS = 2, 3 + K0, 7 + 4 * H

        @block.vector
        def _(dve):
            def norm(n, first):
                s = Steps(dve, ln_step, first)
                for r in range(R):
                    last = dve.bn_stats(stats[:, r, :], xs[:, r, :])
                s.did(last)
                stand(s.sem, s.start + s.n)
                for r in range(R):
                    last = dve.bn_aggr(mv[:, r, :], stats[:, r, :])
                last.then_inc(stats_ready, 1)
                dve.wait_ge(sd_ready, n)
                s.did(dve.reciprocal(rstd[:], sd[:]))
                s.settle()
                dve.scalar_tensor_tensor(shift[:], mv[:, :, 0], -1.0, rstd[:], ALU.mult, ALU.mult).then_inc(norm_ready, 1)
                dve.wait_ge(hT_psum, n)
                for c in range(C):
                    last = dve.tensor_copy(hT[:, c, :], ps_e[:, 2 * c:2 * c + 2, :].rearrange("p a n -> p (a n)"))
                last.then_inc(hT_ready, 1)
                stand(hT_ready, n)
                assert s.n == LN_STEPS

            def body():
                for free in (masked, e_used, z_used, o1_used, out_stored):
                    dve.sem_inc(free, 1)
                dve.memset(neg[:], NEG1).then_inc(neg_ready, 1)
                dve.wait_ge(neg_ready, 1)
                with dve.Fori(0, B) as b:
                    dve.wait_ge(x_in, b * 16 + 16)
                    norm(b * 2 + 1, b * (2 * LN_STEPS))
                    with dve.Fori(0, R) as t:
                        n = b * R + t
                        s = Steps(dve, t0_step, n * T0_STEPS)
                        for q in range(K0):
                            for c in range(C):
                                last = dve.tensor_scalar(lhs[:, q, c, :], hT[:, c, bass.ts(t, P)],
                                                         aT[:, c, q:q + 1], None, ALU.mult)
                        last.then_inc(lhs_ready, 1)
                        dve.wait_ge(adj_in, b * (32 * R) + t * 16 + 16)
                        for q in range(K0):
                            last = dve.tensor_scalar(masks[:, q, :], adj_t[:], float(q + 1), None, ALU.is_equal)
                        last.then_inc(masked, 1)
                        s.did(dve.memset(S[:], NEG0))
                        s.settle()
                        dve.wait_ge(masked, b * (2 * R) + t + 1 + 1)
                        for q in range(K0):
                            dve.wait_ge(e_copied, n * K0 + q + 1)
                            s.did(dve.scalar_tensor_tensor(
                                tmp[:], ps_e[:, 2 * (q % 2):2 * (q % 2) + 2, :].rearrange("p a n -> p (a n)"),
                                SLOPE0, tmp[:], ALU.mult, ALU.max))
                            stand(s.sem, s.start + s.n)
                            dve.copy_predicated(S[:], masks[:, q, :], tmp[:]).then_inc(e_used, 1)
                        dve.wait_ge(e_used, n * K0 + K0 + 1)
                        dve.tensor_reduce(nm[:], S[:], AX_X, ALU.max, negate=True).then_inc(m_ready, 1)
                        dve.wait_ge(o_ready, n + 1)
                        s.did(dve.reciprocal(rinv[:], rs[:]))
                        s.settle()
                        s.did(dve.scalar_tensor_tensor(xs[:, bass.ts(t, 1), :].rearrange("p a d -> p (a d)"), ps_o[:, 0:D], rinv[:],
                                                       xs[:, bass.ts(t, 1), :].rearrange("p a d -> p (a d)"), ALU.mult, ALU.add))
                        s.settle()
                        assert s.n == T0_STEPS
                    norm(b * 2 + 2, b * (2 * LN_STEPS) + LN_STEPS)
                    for r in range(R):
                        dve.wait_ge(proj_ready, b * R + r + 1)
                        dve.tensor_copy(hw[:, r, :], ps_e[:, r % 4, 0:WN]).then_inc(proj_used, 1)
                    stand(proj_used, b * R + R)
                    with dve.Fori(0, R) as t:
                        n = b * R + t
                        s = Steps(dve, t1_step, n * T1_STEPS)
                        dve.tensor_copy(hwt[:], hw[:, bass.ts(t, 1), :].rearrange("p a d -> p (a d)")).then_inc(src_ready, 1)
                        dve.wait_ge(src_ready, n + 1)
                        dve.wait_ge(adj_in, b * (32 * R) + t * 16 + (16 * R + 16))
                        for q in range(T1 + 1):
                            last = dve.tensor_scalar(masks[:, q, :], adj_t[:], float(q), None, ALU.is_equal)
                        last.then_inc(masked, 1)
                        dve.wait_ge(masked, b * (2 * R) + t + (R + 1) + 1)
                        dve.wait_ge(out_stored, n * 16 + 1)
                        for h in range(H):
                            nh = n * H + h
                            s.did(dve.memset(S[:], 0.0))
                            for q in range(T1):
                                dve.wait_ge(z_ready, nh * T1 + q + 1)
                                stand(s.sem, s.start + s.n)
                                dve.copy_predicated(S[:], masks[:, q + 1, :], tmp[:]).then_inc(z_used, 1)
                                dve.wait_ge(z_used, nh * T1 + q + 1 + 1)
                            s.did(dve.scalar_tensor_tensor(S[:], S[:], SLOPE1, S[:], ALU.mult, ALU.max))
                            stand(s.sem, s.start + s.n)
                            s.did(dve.copy_predicated(S[:], masks[:, 0, :], neg[:]))
                            s.settle()
                            dve.tensor_reduce(nm[:], S[:], AX_X, ALU.max, negate=True).then_inc(m1_ready, 1)
                            dve.wait_ge(o1_ready, nh + 1)
                            s.did(dve.reciprocal(rinv[:], rs[:]))
                            s.settle()
                            dve.tensor_scalar(ot[:, h * E:(h + 1) * E], ps_o[:, h * E:(h + 1) * E], rinv[:], None,
                                              ALU.mult).then_inc(o1_used, 1)
                        dve.wait_ge(o1_used, n * H + H + 1)
                        s.did(dve.tensor_tensor(ot[:], ot[:], bgb[:, 0, :], ALU.add))
                        s.settle()
                        s.did(dve.scalar_tensor_tensor(ot[:], ot[:], 0.0, hwt[:, 0:D], ALU.max, ALU.add))
                        s.settle()
                        for h in range(H):
                            last = dve.bn_stats(hst[:, h, :], ot[:, h * E:(h + 1) * E])
                        s.did(last)
                        stand(s.sem, s.start + s.n)
                        for h in range(H):
                            last = dve.bn_aggr(hmv[:, h, :], hst[:, h, :])
                        last.then_inc(hst_ready, 1)
                        dve.wait_ge(hsd_ready, n + 1)
                        s.did(dve.reciprocal(hrs[:], hsd[:]))
                        s.settle()
                        for h in range(H):
                            last = dve.tensor_scalar(ot[:, h * E:(h + 1) * E], ot[:, h * E:(h + 1) * E],
                                                     hmv[:, h, 0:1], hrs[:, h:h + 1], ALU.subtract, ALU.mult)
                        s.did(last)
                        s.settle()
                        s.did(dve.tensor_tensor(ot[:], ot[:], bgb[:, 1, :], ALU.mult))
                        s.settle()
                        s.did(dve.tensor_tensor(ot[:], ot[:], bgb[:, 2, :], ALU.add))
                        s.settle()
                        dve.tensor_tensor(ot[:], ot[:], xs[:, bass.ts(t, 1), :].rearrange("p a d -> p (a d)"), ALU.add).then_inc(out_ready, 1)
                        assert s.n == T1_STEPS
            guarded(dve, body)


def need(eng, signal, value):
    if not isinstance(value, int) or value > 0:
        eng.wait_ge(signal, value)


def plain_path(nc, k, ins, out, flag):
    x, adj = ins["x"], ins["adj"]
    ident, identb, aT, wf, bgb, eps, one, half, pick = (
        k[n] for n in ("ident", "identb", "aT", "wf", "bgb", "eps", "one", "half", "pick"))
    with ExitStack() as ctx:
        sb = lambda name, shape, dt=F32: ctx.enter_context(nc.sbuf_tensor("f_" + name, shape, dt))
        pb = lambda name, shape, dt=F32: ctx.enter_context(nc.psum_tensor("f_" + name, shape, dt))
        xs = [sb(f"xs{i}", [P, R, D]) for i in range(2)]
        hf = sb("hf", [P, R, D])
        hs = [sb("hs_" + part, [P, R, D], F32R) for part in HI_LO]
        hT = [sb("hT_" + part, [P, C, N], F32R) for part in HI_LO]
        ahT = [sb("ahT_" + part, [P, C, N], F32R) for part in HI_LO]
        adj_t = [sb(f"adj{i}", [P, N], I32) for i in range(ADJ_RING)]
        off = [sb(f"off{i}", [P, N], BF16) for i in range(ADJ_RING)]
        mT = [sb(f"mT{i}", [P, R, N], U8) for i in range(2)]
        pos = sb("pos", [P, N])
        ps = [sb(f"ps{i}", [P, N]) for i in range(2)]
        rs = [sb(f"rs{i}", [P, 1]) for i in range(2)]
        rinv = sb("rinv", [P, 1])
        nm = sb("nm", [P, R])
        pT = [sb("pT_" + part, [P, R, P], F32R) for part in HI_LO]
        stats0, mv0, var0, rstd0, shift0 = sb("stats0", [P, R, 6]), sb("mv0", [P, R, 2]), sb("var0", [P, R]), sb("rstd0", [P, R]), sb("shift0", [P, R])
        stats1, mv1, var1, rstd1, shift1 = sb("stats1", [P, R, 6]), sb("mv1", [P, R, 2]), sb("var1", [P, R]), sb("rstd1", [P, R]), sb("shift1", [P, R])
        ub_all = sb("ub", [P, H, N])
        ub = [ub_all[:, h, :] for h in range(H)]
        h1 = ub_all[:, 0:2, :].rearrange("p a n -> p (a n)").rearrange("p (r d) -> p r d", r=R)
        h1T = ub_all[:, 2:4, :]
        hw = sb("hw", [P, R, WF])
        hb = sb("hb", [P, R, H, E + 1])
        ends = sb("ends", [P, 2 * H])
        all_ends = sb("all_ends", [P, 2 * H])
        argd, argb, argu, argc = sb("argd", [P, R, H]), sb("argb", [P, R, H]), sb("argu", [P, R, H]), sb("argc", [P, R, H])
        V, U, rest = sb("V", [P, R, H]), sb("U", [P, R, H]), sb("rest", [P, 2, R, H])
        parts = sb("parts", [P, R, 3, H], BF16)
        uT = sb("uT", [3 * H, N], BF16)
        qs = [sb(f"qs{i}", [P, N]) for i in range(Q_RING)]
        nT = sb("nT", [E + 1, N])
        nsum, ninv = sb("nsum", [P, R]), sb("ninv", [P, R])
        y = sb("y", [P, R, D])
        hst = sb("hst", [P, R * H, 6])
        hsum, hdif, hm2, hsq, hvar, hve, hrstd = (sb(n, [P, R * H]) for n in ("hsum", "hdif", "hm2", "hsq", "hvar", "hve", "hrstd"))
        xb = sb("xb", [P, R, D])
        idle = sb("idle", [P, 16])
        idle_p = sb("idle_p", [P, 16])
        turns = count()
        worst = sb("worst", [P, B])
        apart, depth = sb("apart", [P, H]), sb("depth", [P, H])
        spread = sb("spread", [P, B, H])
        good = sb("good", [P, B * (H + 1)])
        bad = sb("bad", [P, 2])
        e_ps = pb("e_ps", [P, 2, 512])
        t_ps = pb("t_ps", [P, 2, 512])
        o_ps = pb("o_ps", [P, 512])
        m_ps = pb("m_ps", [P, N], BF16)
        n_ps = pb("n_ps", [P, 2, 512])
        flat = lambda a: a.rearrange("p a n -> p (a n)")
        spread_in = (n_ps, t_ps, e_ps, t_ps)
        num = lambda: t_ps[:, :, 0:4 * (E + 1)].rearrange("p a (r e) -> p a r e", r=4)

        S = {n: ctx.enter_context(nc.semaphore("f_" + n)) for n in (
            "pT_lo_ready h_lo_early_ready h_lo_late_ready h_hi_ready "
            "x_in adj0_in adj1_in out_stored "
            "e_ready mt_psum pt_psum o_ready hT_psum h1T_psum pj_ready ut_psum ub_psum unit_done head_psum "
            "pos_ready mt_ready p_ready pT_ready h0_ready h1_ready hT_ready h1T_ready hw_ready ex_ready ut_ready ub_ready nT_ready "
            "t_ready x1_ready x1_step ln1_step st0_ready st1_ready sh0_ready sh1_ready ahT_ready ends_ready arg_ready parts_ready "
            "q_ready head_step head_done y_ready hvar_ready yn_ready tail_step arg_step ln_step worst_ready good_step "
            "off_ready var0_ready rstd0_ready var1_ready rstd1_ready all_ready hbias_ready hb_ready xb_ready "
            "hve_ready hrstd_ready yg_ready out_ready bad_ready").split()}
        block = ctx.enter_context(nc.Block())

        def passes(eng, one_pass):
            one_pass(0, 0, True, False, False, True)
            one_pass(1, 1, True, True, False, True)
            last = B - 2 if B % 2 == 0 else B - 1
            if last > 2:
                with eng.Fori(2, last, 2) as g:
                    one_pass(g, 0, True, True, True, True)
                    one_pass(g + 1, 1, True, True, True, True)
            for g in range(max(last, 2), B + 2):
                one_pass(g, g % 2, g < B, g <= B, True, g + 1 < B)

        @block.sync
        def _(sp):
            def load_x(g, p):
                need(sp, S["xb_ready"], g - 1)
                need(sp, S["h1_ready"], g - 1)
                sp.dma_start(xs[p][:], x[g, :, :].rearrange("(r p) d -> p r d", p=P)).then_inc(S["x_in"], 16)

            def one_pass(g, p, do0, do1, do2, more):
                for r in range(R):
                    n = g * R + r
                    if do0:
                        need(sp, S["off_ready"], n - ADJ_RING + 1)
                        sp.dma_start(adj_t[r % ADJ_RING][:], adj[g, r * P:(r + 1) * P, :]).then_inc(S[f"adj{r % ADJ_RING}_in"], 16)
                    if r == 6 and more:
                        load_x(g + 1, 1 - p)
                    if r == 6 and do2:
                        need(sp, S["out_ready"], g - 1)
                        sp.dma_start(out[g - 2, :, :].rearrange("(r p) d -> p r d", p=P), y[:]).then_inc(S["out_stored"], 16)
            load_x(0, 0)
            passes(sp, one_pass)
            sp.wait_ge(S["out_stored"], 16 * B)

        @block.tensor
        def _(pe):
            def turn_h(g, p, c):
                if c == 0:
                    need(pe, S["h0_ready"], g + 1)
                    need(pe, S["t_ready"], g * R)
                else:
                    need(pe, S["ahT_ready"], g * 2 * C + 2)
                for r in range(R):
                    last = pe.transpose(e_ps[:, r // 4, (r % 4) * P:(r % 4 + 1) * P], hf[:, r, c * P:(c + 1) * P], ident[:])
                last.then_inc(S["hT_psum"], 1)

            def turn_mask(g, r, turned_u):
                n = g * R + r
                need(pe, S["off_ready"], n + 1)
                need(pe, S["mt_ready"], n)
                need(pe, S["ut_ready"], turned_u)
                for j in range(R):
                    last = pe.transpose(m_ps[:, j * P:(j + 1) * P], off[r % ADJ_RING][:, j * P:(j + 1) * P], identb[:])
                last.then_inc(S["mt_psum"], 1)

            def scores(g, p, r):
                n = g * R + r
                if r == 5:
                    need(pe, S["ub_ready"], (g - 1) * H + 3)
                if r == 0:
                    need(pe, S["hT_ready"], (g + 1) * 2 * C)
                    need(pe, S["ahT_ready"], (g + 1) * 2 * C)
                need(pe, S["t_ready"], n)
                for half_ in range(2):
                    cols = slice(half_ * 512, (half_ + 1) * 512)
                    for c in range(C):
                        for i, (a, b) in enumerate(PRODUCTS):
                            pe.matmul(e_ps[:, half_, :], ahT[a][:, c, r * P:(r + 1) * P], hT[b][:, c, cols],
                                      start=(c == 0 and i == 0), stop=False)
                    if half_ == 0:
                        need(pe, S["off_ready"], n + 1)
                    last = pe.matmul(e_ps[:, half_, :], identb[:], off[r % ADJ_RING][:, cols], start=False, stop=True)
                last.then_inc(S["e_ready"], 1)

            def turn_p(m, r, heads, spread_):
                need(pe, S["p_ready"], m + 1)
                need(pe, S["pT_lo_ready"], m)
                need(pe, S["head_done"], heads)
                need(pe, S["ub_ready"], spread_)
                for j in range(R):
                    last = pe.transpose(t_ps[:, j // 4, (j % 4) * P:(j % 4 + 1) * P], ps[r % 2][:, j * P:(j + 1) * P], ident[:])
                last.then_inc(S["pt_psum"], 1)

            def sum0(m, g):
                need(pe, S["pT_ready"], m + 1)
                need(pe, S["pT_lo_ready"], m + 1)
                need(pe, S["h_hi_ready"], g + 1)
                need(pe, S["x1_ready"], m)
                for i, (a, b) in enumerate(PRODUCTS):
                    if (a, b) == (0, 1):
                        need(pe, S["h_lo_early_ready"], g + 1)
                        need(pe, S["h_lo_late_ready"], g + 1)
                    for j in range(R):
                        last = pe.matmul(o_ps[:, 0:D], pT[a][:, j, :], hs[b][:, j, :],
                                         start=(i == 0 and j == 0), stop=(i == 2 and j == R - 1))
                last.then_inc(S["o_ready"], 1)

            def turn_h1(g, c):
                if c == 0:
                    need(pe, S["h1_ready"], g + 1)
                    need(pe, S["nT_ready"], g * H)
                else:
                    need(pe, S["h1T_ready"], g * C + 1)
                for r in range(R):
                    last = pe.transpose(n_ps[:, r // 4, (r % 4) * P:(r % 4 + 1) * P], h1[:, r, c * P:(c + 1) * P], ident[:])
                last.then_inc(S["h1T_psum"], 1)

            def project(g):
                need(pe, S["h1T_ready"], g * C + C)
                for r in range(R):
                    if r >= 2:
                        need(pe, S["hw_ready"], g * R + r - 1)
                    for c in range(C):
                        last = pe.matmul(n_ps[:, r % 2, 0:WF], h1T[:, c, r * P:(r + 1) * P], wf[:, c, :],
                                         start=(c == 0), stop=(c == C - 1))
                    last.then_inc(S["pj_ready"], 1)

            def turn_u(g, n):
                need(pe, S["mt_ready"], n)
                need(pe, S["parts_ready"], g + 1)
                for r in range(R):
                    last = pe.transpose(m_ps[0:3 * H, r * P:(r + 1) * P], parts[:, r, :, :].rearrange("p k h -> p (k h)"), identb[:])
                last.then_inc(S["ut_psum"], 1)

            def spread_u(g, m, h):
                if h == 0:
                    need(pe, S["ut_ready"], g + 1)
                    need(pe, S["hw_ready"], g * R + R)
                if h == 1:
                    need(pe, S["pT_lo_ready"], m)
                if h == 2:
                    need(pe, S["t_ready"], min(m + 1, B * R) if isinstance(m, int) else m + 1)
                if h == 3:
                    need(pe, S["ub_ready"], g * H + 2)
                for half_ in range(2):
                    last = pe.matmul(spread_in[h][:, half_, :], pick[:, h, :], uT[:, half_ * 512:(half_ + 1) * 512],
                                     start=True, stop=True)
                last.then_inc(S["ub_psum"], 1)

            def unit(g, u):
                h, j = u // R, u % R
                need(pe, S["q_ready"], g * UNITS + u + 1)
                if u == 0:
                    need(pe, S["hb_ready"], g + 1)
                    need(pe, S["ub_ready"], g * H + 1)
                if j == 0:
                    need(pe, S["nT_ready"], g * H + h)
                for half_ in range(2):
                    last = pe.matmul(n_ps[0:E + 1, half_, :], hb[:, j, h, :], qs[u % Q_RING][:, half_ * 512:(half_ + 1) * 512],
                                     start=(j == 0), stop=(j == R - 1))
                last.then_inc(S["unit_done"], 1)

            def turn_head(g, h, m):
                need(pe, S["nT_ready"], g * H + h + 1)
                need(pe, S["pT_lo_ready"], m)
                for i in range(R):
                    last = pe.transpose(num()[:, i // 4, i % 4, :], nT[:, i * P:(i + 1) * P], ident[0:E + 1, 0:E + 1])
                last.then_inc(S["head_psum"], 1)

            def one_pass(g, p, do0, do1, do2, more):
                todo = list(range(UNITS)) if do1 else []

                def units(count_):
                    for _ in range(count_ if todo else 0):
                        unit(g - 1, todo.pop(0))

                for r in range(R):
                    n = g * R + r
                    m = n if do0 or (do1 and r == 0) else B * R
                    before = (do0 and r > 0) or (do1 and r == 0)
                    heads = (g - 1) * H - 1 if r == 0 else (g - 1) * H + max(r - 5, 0)
                    if do0 and r != 4:
                        turn_mask(g, r, g if r > 4 else g - 1)
                    if before:
                        turn_p(n - 1, r - 1 if r else R - 1, heads, (g - 1) * H if r < 5 else g * H)
                    if do1 and r == 4:
                        turn_u(g - 1, n if do0 else B * R)
                    if do0:
                        scores(g, p, r)
                    if do0 and r == 4:
                        turn_mask(g, r, g)
                    if do1 and r == 4:
                        spread_u(g - 1, m, 0)
                        spread_u(g - 1, m, 1)
                    if r == 0 and do2:
                        turn_head(g - 2, H - 1, m)
                    if do1:
                        if r == 2:
                            turn_h1(g - 1, 0)
                        if r == 3:
                            project(g - 1)
                        if r >= 5:
                            turn_head(g - 1, r - 5, m)
                    units(UNIT_PLAN[r][0])
                    if before:
                        sum0(n - 1, g if r else g - 1)
                    if do1 and r == 2:
                        turn_h1(g - 1, 1)
                    if do1 and r == 4:
                        spread_u(g - 1, m, 2)
                        spread_u(g - 1, m, 3)
                    units(UNIT_PLAN[r][1])
                for c in range(C):
                    if more:
                        turn_h(g + 1, 1 - p, c)
                    units(END_PLAN[c])
                assert not todo
            turn_h(0, 0, 0)
            turn_h(0, 0, 1)
            passes(pe, one_pass)

        @block.scalar
        def _(act):
            def norm(g, xt, ht, shift_sig, done, rstd, shift, out_free, free_value, rows):
                if 0 in rows:
                    need(act, shift_sig, g + 1)
                    need(act, out_free, free_value)
                for r in rows:
                    last = act.activation(ht[:, r, :], xt[:, r, :], ACT.Relu, bias=shift[:, r:r + 1], scale=rstd[:, r:r + 1])
                if R - 1 in rows:
                    last.then_inc(done, 1)

            def norm0(g, p, rows):
                if 0 in rows:
                    need(act, S["h_lo_early_ready"], g)
                    need(act, S["h_lo_late_ready"], g)
                norm(g, xs[p], hf, S["sh0_ready"], S["h0_ready"], rstd0, shift0, S["hT_psum"], g * C, rows)

            def split_h(g):
                need(act, S["o_ready"], g * R)
                act.activation(hs[0][:].rearrange("p r d -> p (r d)"), hf[:].rearrange("p r d -> p (r d)"), ACT.Copy)\
                    .then_inc(S["h_hi_ready"], 1)

            def norm1(g, p, rows):
                if 0 in rows:
                    need(act, S["q_ready"], g * UNITS)
                norm(g, xs[p], h1, S["sh1_ready"], S["h1_ready"], rstd1, shift1, S["h1T_psum"], g * C, rows)

            def copy_hT(g, c):
                need(act, S["hT_psum"], g * C + c + 1)
                for half_ in range(2):
                    cols = slice(half_ * 512, (half_ + 1) * 512)
                    act.activation(hT[0][:, c, cols], e_ps[:, half_, :], ACT.Copy)
                    act.activation(ahT[0][:, c, cols], e_ps[:, half_, :], ACT.Copy, scale=aT[:, c, 0:1]).then_inc(S["hT_ready"], 1)

            def positive(n):
                need(act, S["e_ready"], n + 1)
                need(act, S["t_ready"], n)
                act.activation(pos[:], flat(e_ps[:]), ACT.Relu, scale=4.0).then_inc(S["pos_ready"], 1)

            def copy_pT(m):
                need(act, S["pt_psum"], m + 1)
                need(act, S["o_ready"], m)
                act.activation(pT[0][:].rearrange("p j i -> p (j i)"), flat(t_ps[:]), ACT.Copy).then_inc(S["pT_ready"], 1)

            def copy_mT(g, p, r):
                need(act, S["mt_psum"], g * R + r + 1)
                if r == 0:
                    need(act, S["q_ready"], (g - 1) * UNITS)
                act.activation(mT[p][:, :, r * P:(r + 1) * P], m_ps[:].rearrange("p (j i) -> p j i", j=R), ACT.Identity,
                               bias=one[:], scale=1.0 / BIG).then_inc(S["mt_ready"], 1)

            def exponent(n, r):
                need(act, S["t_ready"], n + 1)
                need(act, S["x1_ready"], n - 1)
                act.activation(ps[r % 2][:], ps[r % 2][:], ACT.Exp, bias=nm[:, r:r + 1], scale=-1.0,
                               accum_out=rs[r % 2][:]).then_inc(S["p_ready"], 1)

            def copy_h1T(g, c):
                need(act, S["h1T_psum"], g * C + c + 1)
                act.activation(h1T[:, c, :], flat(n_ps[:]), ACT.Copy).then_inc(S["h1T_ready"], 1)

            def copy_hw(g, rows):
                if 0 in rows:
                    need(act, S["y_ready"], g)
                    need(act, S["hbias_ready"], g)
                for r in rows:
                    need(act, S["pj_ready"], g * R + r + 1)
                    act.activation(hw[:, r, :], n_ps[:, r % 2, 0:WF], ACT.Copy).then_inc(S["hw_ready"], 1)

            def factors(g):
                need(act, S["arg_ready"], g + 1)
                need(act, S["unit_done"], g * UNITS)
                act.activation(U[:], argc[:], ACT.Exp).then_inc(S["ex_ready"], 1)
                act.activation(hb[:, :, :, E], argb[:], ACT.Exp).then_inc(S["ex_ready"], 1)
                act.activation(V[:], argb[:], ACT.Exp, scale=-(1.0 - SLOPE1)).then_inc(S["ex_ready"], 1)

            def copy_uT(g):
                need(act, S["ut_psum"], g + 1)
                act.activation(uT[:], m_ps[0:3 * H, :], ACT.Copy).then_inc(S["ut_ready"], 1)

            def copy_u(g, h):
                if h == 0:
                    need(act, S["q_ready"], g * UNITS)
                need(act, S["ub_psum"], g * H + h + 1)
                act.activation(ub[h], flat(spread_in[h][:]), ACT.Copy).then_inc(S["ub_ready"], 1)

            def copy_head(g, h):
                need(act, S["unit_done"], g * UNITS + (h + 1) * R)
                need(act, S["head_psum"], g * H + h)
                act.activation(nT[:], flat(n_ps[0:E + 1]), ACT.Copy).then_inc(S["nT_ready"], 1)

            def one_pass(g, p, do0, do1, do2, more):
                for r in range(R):
                    n = g * R + r
                    if do0 and r == 1:
                        split_h(g)
                    if (do0 and r > 0) or (do1 and r == 0):
                        copy_pT(n - 1)
                    if more and r == 6:
                        norm0(g + 1, 1 - p, range(0, 5))
                    if do1 and r == 4:
                        copy_uT(g - 1)
                    if do0 and r != 4:
                        copy_mT(g, p, r)
                    if do0:
                        positive(n)
                    if do0 and r == 4:
                        copy_mT(g, p, r)
                    if do1 and r == 1:
                        norm1(g - 1, 1 - p, range(0, 2))
                    if more and r == 6:
                        norm0(g + 1, 1 - p, range(5, R))
                    if do1 and r == 2:
                        copy_h1T(g - 1, 0)
                    if do1 and r == 3:
                        copy_hw(g - 1, range(2))
                    if do1 and r == 4:
                        for h in range(H):
                            copy_u(g - 1, h)
                    if do0:
                        exponent(n, r)
                    if do1 and r == 1:
                        norm1(g - 1, 1 - p, range(2, R))
                    if do1 and r == 2:
                        copy_h1T(g - 1, 1)
                    if do1 and r == 3:
                        copy_hw(g - 1, range(2, R))
                        factors(g - 1)
                    if do1 and 4 <= r < 7:
                        copy_head(g - 1, r - 4)
                if more:
                    copy_hT(g + 1, 0)
                    copy_hT(g + 1, 1)
                if do1:
                    copy_head(g - 1, H - 1)
            norm0(0, 0, range(R))
            copy_hT(0, 0)
            copy_hT(0, 1)
            passes(act, one_pass)

        @block.vector
        def _(dve):
            def stand(signal, value):
                if isinstance(value, int):
                    need(dve, signal, value)
                else:
                    dve.wait_ge(signal, value)
                    dve.memset(idle[:, bass.ts(next(turns) % 16, 1)], 0.0)

            def aggregate(mvx, stx, st_sig, step, value):
                stand(step, value)
                for r in range(R):
                    last = dve.bn_aggr(mvx[:, r, :], stx[:, r, :])
                last.then_inc(st_sig, 1)

            def shifted(g, mvx, rstd, shift, rstd_sig, sh_sig):
                need(dve, rstd_sig, g + 1)
                dve.scalar_tensor_tensor(shift[:], mvx[:, :, 0], -1.0, rstd[:], ALU.mult, ALU.mult).then_inc(sh_sig, 1)

            def stats_of_x(g, p):
                need(dve, S["x_in"], g * 16 + 16)
                need(dve, S["h0_ready"], g)
                for r in range(R):
                    last = dve.bn_stats(stats0[:, r, :], xs[p][:, r, :])
                last.then_inc(S["ln_step"], 1)
                aggregate(mv0, stats0, S["st0_ready"], S["ln_step"], g + 1)

            def scale_hT(g, c):
                for half_ in range(2):
                    cols = slice(half_ * 512, (half_ + 1) * 512)
                    need(dve, S["hT_ready"], (g * C + c) * 2 + half_ + 1)
                    dve.tensor_tensor(hT[1][:, c, cols], e_ps[:, half_, :], hT[0][:, c, cols], ALU.subtract)
                    dve.scalar_tensor_tensor(ahT[1][:, c, cols], e_ps[:, half_, :], aT[:, c, 0:1], ahT[0][:, c, cols],
                                             ALU.mult, ALU.subtract).then_inc(S["ahT_ready"], 1)

            def rest_of_p(m):
                need(dve, S["pT_ready"], m + 1)
                dve.tensor_tensor(pT[1][:].rearrange("p j i -> p (j i)"), flat(t_ps[:]),
                                  pT[0][:].rearrange("p j i -> p (j i)"), ALU.subtract).then_inc(S["pT_lo_ready"], 1)

            def rest_of_h(g):
                need(dve, S["h_hi_ready"], g + 1)
                dve.tensor_tensor(hs[1][:, 0:R // 2, :], hf[:, 0:R // 2, :], hs[0][:, 0:R // 2, :], ALU.subtract).then_inc(S["h_lo_early_ready"], 1)

            def leaky(n, r):
                need(dve, S["pt_psum"], n - 1)
                stand(S["pos_ready"], n + 1)
                dve.tensor_tensor_reduce(ps[r % 2][:], flat(e_ps[:]), pos[:], -SLOPE0, 3.0e38, ALU.add, ALU.min,
                                         nm[:, r:r + 1]).then_inc(S["t_ready"], 1)

            def add0(m, p, r):
                need(dve, S["p_ready"], m + 1)
                dve.reciprocal(rinv[:], rs[r % 2][:]).then_inc(S["x1_step"], 1)
                need(dve, S["o_ready"], m + 1)
                need(dve, S["x1_step"], m + 1)
                dve.scalar_tensor_tensor(xs[p][:, r, :], o_ps[:, 0:D], rinv[:], xs[p][:, r, :], ALU.mult, ALU.add)\
                    .then_inc(S["x1_ready"], 1)
                need(dve, S["x1_ready"], m + 1)
                dve.bn_stats(stats1[:, r, :], xs[p][:, r, :]).then_inc(S["ln1_step"], 1)

            def arguments(g):
                need(dve, S["hw_ready"], g * R + R)
                d = hw[:, :, D + H:WF]
                dve.tensor_reduce(ends[:, 0:H], d.rearrange("p r h -> p h r"), AX_X, ALU.max)
                dve.tensor_reduce(ends[:, H:2 * H], d.rearrange("p r h -> p h r"), AX_X, ALU.min, negate=True).then_inc(S["ends_ready"], 1)
                need(dve, S["all_ready"], g + 1)
                top = all_ends[:, 0:H].unsqueeze(1).broadcast_to([P, R, H])
                dve.tensor_tensor(apart[:], all_ends[:, 0:H], all_ends[:, H:2 * H], ALU.add)
                dve.tensor_tensor(argd[:], d, top, ALU.subtract)
                dve.tensor_tensor(argu[:], hw[:, :, D:D + H], top, ALU.add).then_inc(S["arg_step"], 1)
                need(dve, S["arg_step"], g * 5 + 1)
                dve.tensor_scalar(argb[:], argd[:], -CAP, None, ALU.max)
                dve.tensor_scalar(argc[:], argu[:], 1.0 - SLOPE1, CAP, ALU.mult, ALU.min).then_inc(S["arg_ready"], 1)
                dve.tensor_reduce(depth[:], argu[:].rearrange("p r h -> p h r"), AX_X, ALU.min, negate=True).then_inc(S["good_step"], 1)
                need(dve, S["good_step"], g * 2 + 1)
                dve.scalar_tensor_tensor(spread[:, bass.ds(g, 1), :].rearrange("p o h -> p (o h)"), depth[:], DEPTH, apart[:],
                                         ALU.mult, ALU.max).then_inc(S["good_step"], 1)

            def split_u(g):
                need(dve, S["ex_ready"], g * 3 + 3)
                dve.tensor_copy(parts[:, :, 0, :], U[:]).then_inc(S["arg_step"], 1)
                need(dve, S["arg_step"], g * 5 + 2)
                dve.tensor_tensor(rest[:, 0], U[:], parts[:, :, 0, :], ALU.subtract).then_inc(S["arg_step"], 1)
                need(dve, S["arg_step"], g * 5 + 3)
                dve.tensor_copy(parts[:, :, 1, :], rest[:, 0]).then_inc(S["arg_step"], 1)
                need(dve, S["arg_step"], g * 5 + 4)
                dve.tensor_tensor(rest[:, 1], rest[:, 0], parts[:, :, 1, :], ALU.subtract).then_inc(S["arg_step"], 1)
                need(dve, S["arg_step"], g * 5 + 5)
                dve.tensor_copy(parts[:, :, 2, :], rest[:, 1]).then_inc(S["parts_ready"], 1)

            def weigh(g, p, u):
                h, j = u // R, u % R
                if j == 0:
                    need(dve, S["ub_ready"], g * H + h + 1)
                if u == 0:
                    need(dve, S["mt_ready"], g * R + R)
                need(dve, S["unit_done"], g * UNITS + u - Q_RING + 1)
                dve.scalar_tensor_tensor(qs[u % Q_RING][:], ub[h], V[:, j, h:h + 1], mT[p][:, j, :], ALU.max, ALU.mult)\
                    .then_inc(S["q_ready"], 1)

            def head(g, h):
                need(dve, S["head_psum"], g * H + h + 1)
                dve.tensor_scalar(nsum[:].rearrange("p (a r) -> p a r", a=2), num()[:, :, :, E], TINY, None, ALU.max)\
                    .then_inc(S["head_step"], 1)
                need(dve, S["head_step"], (g * H + h) * 2 + 1)
                dve.reciprocal(ninv[:], nsum[:]).then_inc(S["head_step"], 1)
                if h == 0:
                    need(dve, S["out_stored"], g * 16)
                need(dve, S["head_step"], (g * H + h) * 2 + 2)
                dve.tensor_tensor(y[:, :, h * E:(h + 1) * E].rearrange("p (a r) e -> p a r e", a=2), num()[:, :, :, 0:E],
                                  ninv[:].rearrange("p (a r) -> p a r", a=2).unsqueeze(3).broadcast_to([P, 2, 4, E]), ALU.mult)\
                    .then_inc(S["head_done"], 1)

            def add1(g):
                need(dve, S["head_done"], g * H + H)
                dve.scalar_tensor_tensor(y[:], y[:], 0.0, hw[:, :, 0:D], ALU.max, ALU.add).then_inc(S["y_ready"], 1)

            def tail_stats(g, rows):
                if 0 in rows:
                    need(dve, S["y_ready"], g + 1)
                for i in range(rows[0] * H, (rows[-1] + 1) * H):
                    last = dve.bn_stats(hst[:, i, :], y[:, i // H, (i % H) * E:(i % H + 1) * E])
                if R - 1 in rows:
                    last.then_inc(S["tail_step"], 1)

            def tail_variance(g):
                need(dve, S["tail_step"], g * 4 + 1)
                dve.tensor_tensor(hsum[:], hst[:, :, 1], hst[:, :, 4], ALU.add)
                dve.tensor_tensor(hdif[:], hst[:, :, 1], hst[:, :, 4], ALU.subtract)
                dve.tensor_tensor(hm2[:], hst[:, :, 2], hst[:, :, 5], ALU.add).then_inc(S["tail_step"], 1)
                need(dve, S["tail_step"], g * 4 + 2)
                dve.scalar_tensor_tensor(hsq[:], hdif[:], 0.25, hdif[:], ALU.mult, ALU.mult).then_inc(S["tail_step"], 1)
                need(dve, S["tail_step"], g * 4 + 3)
                dve.scalar_tensor_tensor(hvar[:], hm2[:], 1.0 / E, hsq[:], ALU.mult, ALU.add).then_inc(S["hvar_ready"], 1)

            wide = lambda a: a[:].unsqueeze(2).broadcast_to([P, R * H, E])
            ye = y[:].rearrange("p r (h e) -> p (r h) e", h=H)

            def tail_centre(g):
                dve.scalar_tensor_tensor(ye, wide(hsum), -0.5, ye, ALU.mult, ALU.add).then_inc(S["tail_step"], 1)

            def tail_norm(g):
                need(dve, S["hrstd_ready"], g + 1)
                need(dve, S["tail_step"], g * 4 + 4)
                dve.tensor_tensor(ye, ye, wide(hrstd), ALU.mult).then_inc(S["yn_ready"], 1)

            def one_pass(g, p, do0, do1, do2, more):
                todo = list(range(UNITS)) if do1 else []

                def units(count_):
                    for _ in range(count_ if todo else 0):
                        weigh(g - 1, 1 - p, todo.pop(0))

                for r in range(R):
                    n = g * R + r
                    if (do0 and r > 2) or (do1 and r == 0):
                        rest_of_p(n - 1)
                    units(UNIT_PLAN[r][0])
                    if do0:
                        leaky(n, r)
                    if do1 and r >= 5:
                        head(g - 1, r - 5)
                    if do2 and r == 0:
                        head(g - 2, H - 1)
                    if do2 and r == 1:
                        add1(g - 2)
                    if do2 and r == 2:
                        tail_stats(g - 2, range(4, R))
                    if do2 and r == 3:
                        tail_norm(g - 2)
                    ahead = min(UNIT_PLAN[r][1], Q_RING) if r < R - 1 else len(todo)
                    units(ahead)
                    if do1 and r == 3:
                        arguments(g - 1)
                        split_u(g - 1)
                    if (do0 and r > 0) or (do1 and r == 0):
                        add0(n - 1, p if r else 1 - p, r - 1 if r else R - 1)
                    if do1 and r == 0:
                        aggregate(mv1, stats1, S["st1_ready"], S["ln1_step"], g * R)
                    if do0 and r == 0:
                        rest_of_h(g)
                        rest_of_p(n)
                    if do1 and r == 0:
                        shifted(g - 1, mv1, rstd1, shift1, S["rstd1_ready"], S["sh1_ready"])
                    if do2 and r == 1:
                        tail_stats(g - 2, range(0, 4))
                    if do0 and r == 1:
                        rest_of_p(n)
                    if do2 and r == 2:
                        tail_variance(g - 2)
                        tail_centre(g - 2)
                    if r == 5 and more:
                        stats_of_x(g + 1, 1 - p)
                    units(UNIT_PLAN[r][1] - ahead if r < R - 1 else 0)
                    if r == 5 and more:
                        shifted(g + 1, mv0, rstd0, shift0, S["rstd0_ready"], S["sh0_ready"])
                if do0:
                    stand(S["t_ready"], g * R + R)
                    dve.tensor_reduce(worst[:, bass.ds(g, 1)], nm[:], AX_X, ALU.max, apply_absolute_value=True)\
                        .then_inc(S["worst_ready"], 1)
                for c in range(C):
                    if more:
                        scale_hT(g + 1, c)
            stats_of_x(0, 0)
            shifted(0, mv0, rstd0, shift0, S["rstd0_ready"], S["sh0_ready"])
            scale_hT(0, 0)
            scale_hT(0, 1)
            passes(dve, one_pass)
            dve.wait_ge(S["worst_ready"], B)
            dve.wait_ge(S["good_step"], 2 * B)
            dve.tensor_scalar(good[:, 0:B], worst[:], LIMIT, None, ALU.is_lt)
            dve.tensor_scalar(good[:, B:], spread[:].rearrange("p g h -> p (g h)"), SPREAD, None, ALU.is_le).then_inc(S["good_step"], 1)
            dve.wait_ge(S["good_step"], 2 * B + 1)
            dve.tensor_reduce(bad[:, 0:1], good[:], AX_X, ALU.min).then_inc(S["good_step"], 1)
            dve.wait_ge(S["good_step"], 2 * B + 2)
            dve.tensor_scalar(bad[:, 0:1], bad[:, 0:1], -1.0, 1.0, ALU.mult, ALU.add).then_inc(S["good_step"], 1)
            dve.wait_ge(S["bad_ready"], 1)
            dve.tensor_copy(flag, bad[0:1, 1:2])

        @block.gpsimd
        def _(pool):
            def stand(signal, value):
                if isinstance(value, int):
                    need(pool, signal, value)
                else:
                    pool.wait_ge(signal, value)
                    pool.tensor_tensor(idle_p[:, bass.ts(next(turns) % 16, 1)], one[:], one[:], ALU.add)

            def inverse_root(g, var, eps_col, signal, ve, ve_ready, out_, ready, n):
                need(pool, signal, g + 1)
                pool.tensor_tensor(ve[:], var, eps[:, eps_col:eps_col + 1].broadcast_to([P, n]), ALU.add).then_inc(ve_ready, 1)
                need(pool, ve_ready, g + 1)
                pool.tensor_tensor(out_[:], ve[:], half[:, 0:n], ALU.pow).then_inc(ready, 1)

            def rest_of_h(g):
                need(pool, S["h_hi_ready"], g + 1)
                pool.tensor_tensor(hs[1][:, R // 2:, :], hf[:, R // 2:, :], hs[0][:, R // 2:, :], ALU.subtract)\
                    .then_inc(S["h_lo_late_ready"], 1)

            def root0(g):
                inverse_root(g, mv0[:, :, 1], 0, S["st0_ready"], var0, S["var0_ready"], rstd0, S["rstd0_ready"], R)

            def missing(n, g, r):
                need(pool, S["e_ready"], n - ADJ_RING + 1)
                need(pool, S["mt_psum"], n - ADJ_RING + 1)
                stand(S[f"adj{r % ADJ_RING}_in"], g * (16 * R // ADJ_RING) + (r // ADJ_RING + 1) * 16)
                pool.tensor_scalar(off[r % ADJ_RING][:], adj_t[r % ADJ_RING][:].bitcast(U32), BIG, -BIG, ALU.mult, ALU.add)\
                    .then_inc(S["off_ready"], 1)

            by_head = lambda a: a.rearrange("p r (h e) -> p r h e", h=H)
            over_rows = lambda i: bgb[:, i, :].unsqueeze(1).broadcast_to([P, R, D])

            def ends_all(g):
                stand(S["ends_ready"], g + 1)
                pool.partition_all_reduce(all_ends[:], ends[:], P, bass.bass_isa.ReduceOp.max).then_inc(S["all_ready"], 1)

            def add_bias(g):
                need(pool, S["unit_done"], g * UNITS)
                need(pool, S["hw_ready"], g * R + R)
                pool.tensor_tensor(hb[:, :, :, 0:E], by_head(hw[:, :, 0:D]), by_head(over_rows(0)), ALU.add).then_inc(S["hbias_ready"], 1)

            def weigh_h(g):
                need(pool, S["ex_ready"], g * 3 + 2)
                need(pool, S["hbias_ready"], g + 1)
                pool.tensor_tensor(hb[:, :, :, 0:E], hb[:, :, :, 0:E], hb[:, :, :, E:E + 1].broadcast_to([P, R, H, E]), ALU.mult)\
                    .then_inc(S["hb_ready"], 1)

            def residual(g, p):
                need(pool, S["out_ready"], g)
                need(pool, S["x1_ready"], g * R + R)
                pool.tensor_tensor(xb[:], xs[p][:], over_rows(2), ALU.add).then_inc(S["xb_ready"], 1)

            def tail_gamma(g):
                need(pool, S["yn_ready"], g + 1)
                pool.tensor_tensor(y[:], y[:], over_rows(1), ALU.mult).then_inc(S["yg_ready"], 1)

            def tail_add(g):
                need(pool, S["yg_ready"], g + 1)
                need(pool, S["xb_ready"], g + 1)
                pool.tensor_tensor(y[:], y[:], xb[:], ALU.add).then_inc(S["out_ready"], 1)

            def one_pass(g, p, do0, do1, do2, more):
                for r in range(R):
                    n = g * R + r
                    if do0 and (r + 1 < R or more):
                        missing(n + 1, g if r + 1 < R else g + 1, (r + 1) % R)
                    if do1 and r == 0:
                        inverse_root(g - 1, mv1[:, :, 1], 0, S["st1_ready"], var1, S["var1_ready"], rstd1, S["rstd1_ready"], R)
                    if do0 and r == 0:
                        rest_of_h(g)
                    if do2 and r == 2:
                        inverse_root(g - 2, hvar[:], 1, S["hvar_ready"], hve, S["hve_ready"], hrstd, S["hrstd_ready"], R * H)
                    if do1 and r == 3:
                        ends_all(g - 1)
                        add_bias(g - 1)
                        weigh_h(g - 1)
                    if do2 and r == 4:
                        tail_gamma(g - 2)
                        tail_add(g - 2)
                    if do1 and r == 4:
                        residual(g - 1, 1 - p)
                    if more and r == 5:
                        root0(g + 1)
            root0(0)
            missing(0, 0, 0)
            passes(pool, one_pass)
            pool.wait_ge(S["good_step"], 2 * B + 3)
            pool.partition_all_reduce(bad[:, 1:2], bad[:, 0:1], P, bass.bass_isa.ReduceOp.max).then_inc(S["bad_ready"], 1)


def program(nc, ins, out):
    with ExitStack() as ctx:
        k = constants(nc, ctx, ins)
        flag = ctx.enter_context(nc.sbuf_tensor("flag", [1, 1], I32))[:]
        plain_path(nc, k, ins, out, flag)
        general_path(nc, k, ins, out, flag)


_INS = ["x", "adj", "L0_gnn_a_0", "L0_gnn_a_1", "L0_gnn_a_2", "L0_gnn_a_3", "L1_gnn_W", "L1_gnn_a_src",
        "L1_gnn_a_dst", "L1_gnn_bias", "L1_gnn_ln_gamma", "L1_gnn_ln_beta"]


def kernel(**inputs):
    import numpy as _np
    import concourse.bacc as _bacc
    from concourse import mybir as _mybir
    from concourse.bass_utils import run_bass_kernel_spmd as _run

    nc = _bacc.Bacc("TRN2", target_bir_lowering=False, num_devices=1)
    arrays, aps = {}, {}
    for name in _INS:
        a = _np.ascontiguousarray(inputs[name])
        arrays[f"in_{name}"] = a
        aps[name] = nc.dram_tensor(f"in_{name}", a.shape, _mybir.dt.from_np(a.dtype), kind="ExternalInput").ap()
    out = nc.dram_tensor("out_0", (B, N, D), F32, kind="ExternalOutput").ap()
    program(nc, aps, out)
    r = _run(nc, [arrays], core_ids=[0])
    return r.results[0]["out_0"]
```
